# Optimizing a Trainium2 kernel written in Bass

```python
import numpy as np
import jax
import jax.numpy as jnp

def _softmax(x, axis=-1):
    return jax.nn.softmax(x, axis=axis)

def _gelu(x):
    return jax.nn.gelu(x, approximate=True)

def _silu(x):
    return jax.nn.silu(x)

def _sigmoid(x):
    return jax.nn.sigmoid(x)

def _layernorm(x, axis=-1, eps=1e-05):
    m = jnp.mean(x, axis=axis, keepdims=True)
    v = jnp.var(x, axis=axis, keepdims=True)
    return (x - m) / jnp.sqrt(v + eps)

def _scatter_add(tgt, idx, src, axis=0):
    return tgt.at[idx].add(src)

def _segment_sum(src, seg, n):
    return jax.ops.segment_sum(src, seg, n)
kernel_name = 'mk_adj_preln_d2_adj_r2_1d5219'

def setup_inputs(seed: int=0):
    np.random.seed(seed)
    _w = jnp.asarray

    def _rec_inputs():
        import jax
        import jax.numpy as jnp
        _gk = jax.random.key(seed)
        x = -0.0002928 + 1 * jax.random.normal(jax.random.fold_in(_gk, 1), (2048, 256), jnp.float32)
        _a = jax.random.bernoulli(jax.random.fold_in(_gk, 2), 0.0078125, (2048, 2048))
        _a = jnp.logical_or(_a, jnp.swapaxes(_a, -1, -2))
        _a = jnp.logical_or(_a, jnp.eye(2048, dtype=bool))
        _af = _a.astype(jnp.float32)
        _af = _af * jax.random.uniform(jax.random.fold_in(_gk, 3), (2048, 2048), jnp.float32, 0.05, 1000000000.0)
        adj = _af
        return (x, adj)
    x, adj = _rec_inputs()

    def _L0_gnn_setup():
        import jax, jax.numpy as jnp
        import numpy as np
        N_HEADS = 4
        N_HIDDEN = 256
        SLOPE = 0.01
        NEG = -1000000000.0
        key = jax.random.key(seed)
        k1, k2, k3, k4 = jax.random.split(key, 4)
        N, F_IN = (4096, 256)
        h = jax.random.normal(k1, (N, F_IN), dtype=jnp.float32)
        W = jax.random.normal(k2, (F_IN, N_HIDDEN * N_HEADS), dtype=jnp.float32) * 0.05
        a = jax.random.normal(k3, (N_HEADS, 2 * N_HIDDEN, 1), dtype=jnp.float32) * 0.05
        adj_mat = jnp.where(jax.random.uniform(k4, (N, N)) < 0.01, 0.0, NEG).astype(jnp.float32)
        return {'h': h, 'adj_mat': adj_mat, 'W': W, 'a': a}
    _L0_gnn_all = _L0_gnn_setup()
    _L0_gnn_in = {k: v for k, v in _L0_gnn_all.items() if k in ('W', 'a')}
    del _L0_gnn_all

    def _L1_gnn_setup():
        import jax, jax.numpy as jnp
        import numpy as np
        N = 4096
        F_IN = 256
        F_OUT = 256
        DENSITY = 0.01
        key = jax.random.key(seed)
        k_x, k_adj, k_w, k_b = jax.random.split(key, 4)
        input_features = jax.random.normal(k_x, (N, F_IN), dtype=jnp.float32)
        adj = (jax.random.uniform(k_adj, (N, N)) < DENSITY).astype(jnp.float32)
        idx = jnp.arange(N)
        adj = adj.at[idx, idx].set(1.0)
        W = jax.random.normal(k_w, (F_IN, F_OUT), dtype=jnp.float32) / np.sqrt(F_IN)
        b = jax.random.normal(k_b, (F_OUT,), dtype=jnp.float32) * 0.01
        return {'input_features': input_features, 'adj': adj, 'W': W, 'b': b}
    _L1_gnn_all = _L1_gnn_setup()
    _L1_gnn_in = {k: v for k, v in _L1_gnn_all.items() if k in ('W', 'b')}
    del _L1_gnn_all
    return {'x': x, 'adj': adj, 'L0_gnn_W': _L0_gnn_in['W'], 'L0_gnn_a': _L0_gnn_in['a'], 'L1_gnn_W': _L1_gnn_in['W'], 'L1_gnn_b': _L1_gnn_in['b']}

def reference(x, adj, L0_gnn_W, L0_gnn_a, L1_gnn_W, L1_gnn_b):
    import jax
    import jax.numpy as jnp

    def _L0_gnn_ref(h, adj_mat, W, a):
        import jax, jax.numpy as jnp
        import numpy as np
        N_HEADS = 4
        N_HIDDEN = 256
        SLOPE = 0.01
        NEG = -1000000000.0
        N = h.shape[0]
        ht = (h @ W).reshape(N, N_HEADS, N_HIDDEN).transpose(1, 0, 2)
        a_src = a[:, :N_HIDDEN, 0]
        a_dst = a[:, N_HIDDEN:, 0]
        src = jnp.einsum('hnd,hd->hn', ht, a_src)
        dst = jnp.einsum('hnd,hd->hn', ht, a_dst)
        e = jax.nn.leaky_relu(src[:, :, None] + dst[:, None, :], SLOPE) + adj_mat[None]
        att = jax.nn.softmax(e, axis=-1)
        h_prime = jnp.einsum('hij,hjd->hid', att, ht)
        return h_prime.mean(axis=0)

    def _L1_gnn_ref(input_features, adj, W, b):
        import jax, jax.numpy as jnp
        import numpy as np
        N = 4096
        F_IN = 256
        F_OUT = 256
        DENSITY = 0.01
        A = (adj != 0).astype(input_features.dtype)
        hidden = input_features @ W + b
        deg = jnp.sum(A, axis=0)
        return A @ hidden / deg[:, None]
    h = jnp.maximum(_layernorm(x, axis=-1), 0.0)
    x = x + _L0_gnn_ref(h, adj, L0_gnn_W, L0_gnn_a)
    h = jnp.maximum(_layernorm(x, axis=-1), 0.0)
    x = x + _L1_gnn_ref(h, adj, L1_gnn_W, L1_gnn_b)
    return x

_drawn_inputs = setup_inputs


def setup_inputs(seed=0):
    import zlib

    import numpy as np

    out = dict(_drawn_inputs(seed))
    spreads = {}
    factors = {'L1_gnn_b': 6.897}
    for name, (base, spread) in spreads.items():
        noise = np.random.default_rng([zlib.crc32(name.encode()), seed]).standard_normal(out[name].shape)
        drawn = base * np.exp(spread * noise) if base else spread * noise
        out[name] = jnp.asarray(drawn.astype(out[name].dtype))
    for name, factor in factors.items():
        out[name] = (out[name] * factor).astype(out[name].dtype)
    return out
```

```python
from contextlib import ExitStack

import concourse.bass as bass
from concourse import mybir

P = 128
N = 2048
F = 256
HEADS = 4
NB = N // P
FK = F // P
UNITS = NB * HEADS
CH = N // 2
CB = CH // P
SLOPE = 0.01
EPS = 1e-5


def gnn_kernel(nc, x, adj, w0, a0, w1, b1, out):
    fp32 = mybir.dt.float32
    f32r = mybir.dt.float32r
    u8 = mybir.dt.uint8
    ALU = mybir.AluOpType
    ACT = mybir.ActivationFunctionType

    x1_dram = nc.dram_tensor("x1_scratch", (N, F), fp32, kind="Internal").ap()
    hid_dram = nc.dram_tensor("hidden_scratch", (N, F), fp32, kind="Internal").ap()

    def blocks(t):
        return t.rearrange("(b p) f -> p b f", p=P)

    ctx = ExitStack()
    with ctx:
        where = {"": (nc.sbuf_base + 63) // 64 * 64}

        def size(shape, dt):
            n = 1
            for s in shape[1:]:
                n *= s
            return n * {fp32: 4, f32r: 4, u8: 1}[dt]

        def place(name, shape, dt):
            at = where[""]
            where[name] = at
            where[""] = at + (size(shape, dt) + 31) // 32 * 32
            assert where[""] <= nc.sbuf_usable_end, name
            return nc.alloc_sbuf_tensor_at(name, shape, dt, offset=at)

        def alias(name, shape, dt, over, skip=0):
            return nc.alloc_sbuf_tensor_at(name, shape, dt, offset=where[over] + skip)

        D = place("dst_rows", [P, HEADS, N], fp32)
        AT = place("mask_t", [P, NB, N], u8)
        H = place("h_split", [P, NB, 2 * F], f32r)
        W = place("w0_split", [P, FK, HEADS, 2 * F], f32r)
        E = place("logits", [P, 2, N], fp32)
        B = place("adj_dst", [P, 2, N], fp32)
        ADJ = place("adj_rows", [P, N], fp32)
        PT = place("probs_t", [P, 4, 2, CH], f32r)
        U = place("u_rows", [P, F], fp32)
        UH = place("u_half", [P, F], fp32)
        UT = place("u_t", [P, 2, F], f32r)
        W1 = place("w1", [P, FK, F], fp32)
        B1 = place("b1_rows", [P, F], fp32)
        XR = place("x_res", [P, F], fp32)
        XS = place("x_sum", [P, F], fp32)
        X1 = place("x1", [P, F], fp32)
        HN1 = place("x1_norm", [P, F], fp32)
        HT1 = place("h1_t", [P, FK, P], fp32)
        HID = place("hidden", [P, F], fp32)
        ident = place("ident", [P, P], fp32)
        src = place("src_bias", [P, UNITS], fp32)
        nmax = place("neg_max", [P, HEADS], fp32)
        rsum = place("row_sum", [P, HEADS], fp32)
        rinv = place("row_inv", [P, HEADS], fp32)
        stat = place("stat", [P, 6], fp32)
        mv = place("mean_var", [P, 2], fp32)
        veps = place("var_eps", [P, 1], fp32)
        rstd = place("rstd", [P, 1], fp32)
        power = place("power", [P, NB], fp32)
        deg = place("deg", [P, NB], fp32)
        rdeg = place("rdeg", [P, NB], fp32)

        XA = alias("x_all", [P, NB, F], fp32, "logits")
        WR = alias("w0_raw", [P, FK, HEADS, F], fp32, "adj_dst")
        AB = alias("a_rows", [P, HEADS, 2 * F], fp32, "adj_dst", 4 * N)
        HT = alias("h_t", [P, FK, N], fp32, "probs_t")
        o = 4 * FK * N
        WDB = alias("wa_dst_cols", [P, FK, HEADS, P], fp32, "probs_t", o)
        o += 4 * FK * HEADS * P
        WA = alias("wa", [P, FK, 2, HEADS], fp32, "probs_t", o)
        o += 4 * FK * 2 * HEADS
        JUNK = alias("junk", [P, F], fp32, "probs_t", o)
        o += 4 * F
        ST = alias("x_stats", [P, NB, 6], fp32, "probs_t", o)
        o += 4 * NB * 6
        LN = alias("ln_terms", [P, 8, NB], fp32, "probs_t", o)
        HIN = alias("hidden_in", [P, NB, F], fp32, "logits")
        X1R = alias("x1_in", [P, NB, F], fp32, "adj_dst")
        OH = alias("out_half", [P, 2, F], fp32, "adj_rows")
        OS = alias("out_sum", [P, 2, F], fp32, "adj_rows", 8 * F)
        OUT = alias("out_rows", [P, 2, F], fp32, "adj_rows", 16 * F)

        def psum(name, cols):
            return ctx.enter_context(nc.psum_tensor(name, [P, cols], fp32))

        PP = [psum(f"ps_chunk{i}", CH) for i in range(2)]
        ACC = [psum(f"ps_acc{i}", 2 * F) for i in range(2)]
        PO = psum("ps_out", 2 * F)
        PM = psum("ps_misc", 2 * F)

        def sem(name):
            return ctx.enter_context(nc.semaphore(name))

        x_in = [sem(f"x_in{g}") for g in range(4)]
        w0_in, a0_in, w1_in, b1_in = sem("w0_in"), sem("a0_in"), sem("w1_in"), sem("b1_in")
        adj_in, xres_in = sem("adj_in"), sem("xres_in")
        x1_stored, hid_stored = sem("x1_stored"), sem("hid_stored")
        hid_in, x1_in, out_stored = sem("hid_in"), sem("x1_in"), [sem("out_stored0"), sem("out_stored1")]
        zeroed, ident_ready, power_ready = sem("zeroed"), sem("ident_ready"), sem("power_ready")
        vec_step = sem("vec_step")
        stats_ready, x_rstd_ready = sem("stats_ready"), sem("x_rstd_ready")
        norm_ready, h_hi_ready, h_lo_ready = sem("norm_ready"), sem("h_hi_ready"), sem("h_lo_ready")
        h_transposed, ht_ready = sem("h_transposed"), sem("ht_ready")
        wa_ready, wdb_ready, w_hi_ready, w_lo_ready = sem("wa_ready"), sem("wdb_ready"), sem("w_hi_ready"), sem("w_lo_ready")
        src_summed, src_ready, d_summed, d_ready = sem("src_summed"), sem("src_ready"), sem("d_summed"), sem("d_ready")
        adj_dst_ready = sem("adj_dst_ready")
        relu_ready = sem("relu_ready")
        logits_ready = sem("logits_ready")
        probs_ready = sem("probs_ready")
        rinv_ready = sem("rinv_ready")
        chunk_transposed = sem("chunk_transposed")
        hi_ready, lo_ready = sem("hi_ready"), sem("lo_ready")
        chunk_multiplied = sem("chunk_multiplied")
        half_ready, u_ready = sem("half_ready"), sem("u_ready")
        u_transposed, ut_hi_ready, ut_lo_ready = sem("u_transposed"), sem("ut_hi_ready"), sem("ut_lo_ready")
        w_multiplied = sem("w_multiplied")
        adj_transposed, mask_ready = sem("adj_transposed"), sem("mask_ready")
        x_sum_ready, x1_ready, stat_ready, mv_ready, veps_ready, rstd_ready = (
            sem("x_sum_ready"), sem("x1_ready"), sem("stat_ready"), sem("mv_ready"),
            sem("veps_ready"), sem("rstd_ready"))
        norm1_ready, h1_transposed, h1_ready, hid_summed, hid_ready = (
            sem("norm1_ready"), sem("h1_transposed"), sem("h1_ready"), sem("hid_summed"),
            sem("hid_ready"))
        hid_hi_ready, hid_lo_ready = sem("hid_hi_ready"), sem("hid_lo_ready")
        cast_ready, out_summed, out_half_ready = sem("cast_ready"), sem("out_summed"), sem("out_half_ready")
        deg_ready, rdeg_ready, out_sum_ready, out_ready = (
            sem("deg_ready"), sem("rdeg_ready"), sem("out_sum_ready"), sem("out_ready"))
        passed_vec, passed_act, passed_pool = sem("passed_vec"), sem("passed_act"), sem("passed_pool")

        HSPLIT = [(0, 5), (5, 10), (10, 15)]

        def has(u):
            return not isinstance(u, int) or 0 <= u < UNITS

        def block_loop(eng, body, first=2):
            for ib in range(first):
                body(ib)
            with eng.Fori(first, NB - 1) as ib:
                body(ib)
            body(NB - 1)

        def final(ib):
            return isinstance(ib, int) and ib == NB - 1

        block = ctx.enter_context(nc.Block())

        @block.sync
        def _(sp):
            for g in range(4):
                sp.dma_start(XA[:, 4 * g:4 * g + 4, :], blocks(x)[:, 4 * g:4 * g + 4, :]).then_inc(x_in[g], 16)
            sp.dma_start(AB[:, :, :].rearrange("p h d -> p (h d)"), a0.rearrange("h d o -> (h d o)").partition_broadcast(P)).then_inc(a0_in, 16)
            sp.dma_start(WR[:, :, :, :], w0.rearrange("(k p) (h d) -> p k h d", p=P, h=HEADS)).then_inc(w0_in, 16)
            sp.dma_start(ADJ[:, :], adj[0:P, :]).then_inc(adj_in, 16)
            sp.dma_start(W1[:, :, :], w1.rearrange("(k p) f -> p k f", p=P)).then_inc(w1_in, 16)
            sp.dma_start(B1[:, :], b1.partition_broadcast(P)).then_inc(b1_in, 16)

            def store_hidden(b):
                sp.wait_ge(hid_ready, b + 1)
                sp.dma_start(hid_dram[bass.ds(b * P, P), :], HID[:, :]).then_inc(hid_stored, 16)

            def store_x1(b):
                sp.wait_ge(x1_ready, b + 1)
                sp.dma_start(x1_dram[bass.ds(b * P, P), :], X1[:, :]).then_inc(x1_stored, 16)

            def body(ib):
                if not final(ib):
                    sp.wait_ge(adj_dst_ready, 4 * ib + 4)
                    sp.wait_ge(adj_transposed, 2 * ib + 2)
                    sp.dma_start(ADJ[:, :], adj[bass.ds((ib + 1) * P, P), :]).then_inc(adj_in, 16)
                if not isinstance(ib, int) or ib >= 2:
                    store_hidden(ib - 2)
                if not isinstance(ib, int) or ib >= 1:
                    store_x1(ib - 1)
                sp.dma_start(XR[:, :], x[bass.ds(ib * P, P), :]).then_inc(xres_in, 16)
            block_loop(sp, body)
            store_hidden(NB - 2)
            store_x1(NB - 1)
            sp.wait_ge(hid_stored, 16 * (NB - 1))
            sp.wait_ge(chunk_transposed, 2 * UNITS)
            sp.dma_start(HIN[:, 0:NB - 1, :], blocks(hid_dram)[:, 0:NB - 1, :]).then_inc(hid_in, 16)
            sp.wait_ge(x1_stored, 16 * NB)
            sp.wait_ge(logits_ready, UNITS)
            sp.dma_start(X1R[:, :, :], blocks(x1_dram)).then_inc(x1_in, 16)

            def store(ib, j):
                sp.wait_ge(out_ready, ib + 1)
                sp.dma_start(out[bass.ds(ib * P, P), :], OUT[:, j, :]).then_inc(out_stored[j], 16)
            with sp.Fori(0, NB // 2) as pair:
                for j in range(2):
                    store(2 * pair + j, j)
            for j in range(2):
                sp.wait_ge(out_stored[j], 8 * NB)

        @block.gpsimd
        def _(pool):
            nc.gpsimd.memset(ident[:, :], 0.0).then_inc(zeroed, 1)
            nc.gpsimd.memset(power[:, :], -0.5).then_inc(power_ready, 1)
            pool.wait_ge(zeroed, 1)
            nc.gpsimd.affine_select(out=ident[:, :], in_=ident[:, :], compare_op=ALU.not_equal, fill=1.0,
                                    base=0, pattern=[[-1, P]], channel_multiplier=1).then_inc(ident_ready, 1)
            pool.wait_ge(power_ready, 1)
            pool.wait_ge(stats_ready, 1)
            nc.gpsimd.tensor_tensor(LN[:, 7, :], LN[:, 6, :], power[:, :], ALU.pow).then_inc(x_rstd_ready, 1)

            def adj_dst(ib, h):
                u = 4 * ib + h
                if h == 0:
                    pool.wait_ge(adj_in, 16 * (ib + 1))
                if isinstance(u, int) and u < HEADS:
                    pool.wait_ge(d_ready, 2 * h + 2)
                if not isinstance(u, int) or u >= 2:
                    pool.wait_ge(logits_ready, u - 1)
                    pool.sem_inc(passed_pool, 1)
                elif u == 0:
                    pool.wait_ge(w_lo_ready, 1)
                    pool.wait_ge(wa_ready, 1)
                nc.gpsimd.tensor_tensor(B[:, h % 2, :], ADJ[:, :], D[:, h, :], ALU.add).then_inc(adj_dst_ready, 1)

            def rstd_of(b):
                pool.wait_ge(veps_ready, b + 1)
                pool.sem_inc(passed_pool, 1)
                nc.gpsimd.tensor_tensor(rstd[:, :], veps[:, :], power[:, 0:1], ALU.pow).then_inc(rstd_ready, 1)

            def body(ib):
                adj_dst(ib, 0)
                if not isinstance(ib, int) or ib >= 2:
                    rstd_of(ib - 2)
                for h in range(1, HEADS):
                    adj_dst(ib, h)
            block_loop(pool, body)
            rstd_of(NB - 2)
            rstd_of(NB - 1)

        @block.scalar
        def _(act):
            for g in range(4):
                act.wait_ge(norm_ready, 4 * g + 4)
                nc.scalar.activation(H[:, 4 * g:4 * g + 4, 0:F], XA[:, 4 * g:4 * g + 4, :],
                                     ACT.Relu).then_inc(h_hi_ready, 1)
            for g in range(4):
                act.wait_ge(h_transposed, g + 1)
                nc.scalar.activation(
                    HT[:, :, 4 * g * P:(4 * g + 4) * P].rearrange("p k (b c) -> p b k c", b=4),
                    PP[g % 2][:, :].rearrange("p (b k c) -> p b k c", b=4, k=FK),
                    ACT.Relu).then_inc(ht_ready, 1)
            act.wait_ge(src_summed, 1)
            nc.scalar.activation(src[:, :], PM[:, 0:UNITS], ACT.Copy, scale=-(1.0 - SLOPE)).then_inc(src_ready, 1)
            for n in range(2 * HEADS):
                act.wait_ge(d_summed, n + 1)
                nc.scalar.activation(D[:, n // 2, (n % 2) * CH:(n % 2 + 1) * CH], PP[n % 2][:, :],
                                     ACT.Copy).then_inc(d_ready, 1)

            def relu_term(u, h):
                if isinstance(u, int) and u < 2:
                    if u == 0:
                        act.wait_ge(src_ready, 1)
                        act.wait_ge(h_lo_ready, 4)
                else:
                    act.wait_ge(chunk_transposed, 2 * u - 2)
                if isinstance(u, int) and u < HEADS:
                    act.wait_ge(d_ready, 2 * u + 2)
                if not isinstance(u, int):
                    act.sem_inc(passed_act, 1)
                nc.scalar.activation(E[:, h % 2, :], D[:, h, :], ACT.Relu, scale=-(1.0 - SLOPE),
                                     bias=src[:, bass.ds(u, 1)]).then_inc(relu_ready, 1)

            def exp(u, h):
                act.wait_ge(logits_ready, u + 1)
                if not isinstance(u, int) or u >= HEADS:
                    act.wait_ge(rinv_ready, u - HEADS + 1)
                nc.scalar.activation(E[:, h % 2, :], E[:, h % 2, :], ACT.Exp, scale=-1.0,
                                     bias=nmax[:, h:h + 1], accum_out=rsum[:, h:h + 1]).then_inc(probs_ready, 1)

            def high(k, n, m):
                if not isinstance(k, int) or k >= 4:
                    act.wait_ge(chunk_multiplied, k - 3)
                act.wait_ge(chunk_transposed, k + 1)
                nc.scalar.activation(PT[:, n, 0, :], PP[m][:, :], ACT.Copy).then_inc(hi_ready, 1)

            def u_half(v, h):
                act.wait_ge(rinv_ready, v + 1)
                if not isinstance(v, int) or v >= 1:
                    act.wait_ge(u_ready, v)
                act.wait_ge(chunk_multiplied, 2 * v + 2)
                nc.scalar.activation(UH[:, :], ACC[h % 2][:, F:2 * F], ACT.Copy,
                                     scale=rinv[:, h:h + 1]).then_inc(half_ready, 1)

            def ut_high(v):
                if not isinstance(v, int) or v >= 1:
                    act.wait_ge(w_multiplied, v)
                act.wait_ge(u_transposed, v + 1)
                nc.scalar.activation(UT[:, 0, :], PM[:, 0:F], ACT.Copy).then_inc(ut_hi_ready, 1)

            def h1_relu(b):
                if not isinstance(b, int) or b >= 1:
                    act.wait_ge(hid_summed, b)
                act.wait_ge(h1_transposed, b + 1)
                nc.scalar.activation(HT1[:, :, :], PM[:, 0:F].rearrange("p (k c) -> p k c", k=FK),
                                     ACT.Relu).then_inc(h1_ready, 1)

            def slot(ib, h):
                u = 4 * ib + h
                m0, m1 = chunk_buffers(h)
                if h == 3 and (not isinstance(ib, int) or ib >= 1):
                    h1_relu(ib - 1)
                if has(u + 1):
                    high(2 * u + 2, (2 * h + 2) % 4, m0)
                if has(u - 1):
                    u_half(u - 1, (h - 1) % 4)
                if has(u + 2):
                    exp(u + 2, (h + 2) % 4)
                if has(u - 1):
                    ut_high(u - 1)
                if has(u + 1):
                    high(2 * u + 3, (2 * h + 3) % 4, m1)
                if has(u + 3):
                    relu_term(u + 3, (h + 3) % 4)

            relu_term(0, 0)
            relu_term(1, 1)
            exp(0, 0)
            exp(1, 1)
            high(0, 0, 1)
            high(1, 1, 0)
            relu_term(2, 2)

            def body(ib):
                for h in range(HEADS):
                    slot(ib, h)
            block_loop(act, body)
            u_half(UNITS - 1, 3)
            ut_high(UNITS - 1)

            def cast(ib, j):
                if not isinstance(ib, int) or ib >= 2:
                    act.wait_ge(out_summed, ib - 1)
                    act.sem_inc(passed_act, 1)
                nc.scalar.activation(PT[:, j, :, :].rearrange("p t (b c) -> p (t b) c", c=P),
                                     AT[:, :, bass.ds(ib * P, P)], ACT.Copy).then_inc(cast_ready, 1)
            act.wait_ge(mask_ready, 2 * NB)
            act.wait_ge(chunk_multiplied, 2 * UNITS)
            cast(0, 0)
            act.wait_ge(hid_in, 16)
            for lo, hi in HSPLIT:
                nc.scalar.activation(H[:, lo:hi, 0:F], HIN[:, lo:hi, :], ACT.Copy).then_inc(hid_hi_ready, 1)
            cast(1, 1)
            h1_relu(NB - 1)
            act.wait_ge(hid_ready, NB)
            nc.scalar.activation(H[:, NB - 1, 0:F], HID[:, :], ACT.Copy).then_inc(hid_hi_ready, 1)

            def out_half(ib, j):
                act.wait_ge(rdeg_ready, ib + 1)
                if not isinstance(ib, int) or ib >= 2:
                    act.wait_ge(out_sum_ready, ib - 1)
                act.wait_ge(out_summed, ib + 1)
                if not isinstance(ib, int):
                    act.sem_inc(passed_act, 1)
                nc.scalar.activation(OH[:, j, :], ACC[j][:, F:2 * F], ACT.Copy,
                                     scale=rdeg[:, bass.ds(ib, 1)]).then_inc(out_half_ready, 1)
            out_half(0, 0)
            cast(2, 0)
            out_half(1, 1)
            cast(3, 1)
            with act.Fori(1, NB // 2 - 1) as pair:
                for j in range(2):
                    out_half(2 * pair + j, j)
                    cast(2 * pair + j + 2, j)
            for j in range(2):
                out_half(NB - 2 + j, j)

        @block.tensor
        def _(pe):
            pe.wait_ge(ident_ready, 1)
            for g in range(4):
                pe.wait_ge(norm_ready, 4 * g + 4)
                if g >= 2:
                    pe.wait_ge(ht_ready, g - 1)
                for b in range(4):
                    for k in range(FK):
                        c = (b * FK + k) * P
                        last = nc.tensor.transpose(PP[g % 2][:, c:c + P], XA[:, 4 * g + b, k * P:(k + 1) * P],
                                                   ident[:, :])
                last.then_inc(h_transposed, 1)
            pe.wait_ge(ht_ready, 4)
            pe.wait_ge(wa_ready, 1)
            for b in range(NB):
                for k in range(FK):
                    last = nc.tensor.matmul(PM[:, 4 * b:4 * b + 4], HT[:, k, b * P:(b + 1) * P], WA[:, k, 0, :],
                                            start=(k == 0), stop=(k == FK - 1))
            last.then_inc(src_summed, 1)
            pe.wait_ge(wdb_ready, 1)
            for n in range(2 * HEADS):
                h, c = n // 2, (n % 2) * CH
                if n >= 2:
                    pe.wait_ge(d_ready, n - 1)
                for q in range(2):
                    for k in range(FK):
                        last = nc.tensor.matmul(PP[n % 2][:, q * 512:(q + 1) * 512], WDB[:, k, h, :],
                                                HT[:, k, c + q * 512:c + (q + 1) * 512],
                                                start=(k == 0), stop=(k == FK - 1))
                last.then_inc(d_summed, 1)

            def adj_chunk(ib, a, m):
                if a == 0:
                    pe.wait_ge(adj_in, 16 * (ib + 1))
                for j in range(CB):
                    c = a * CH + j * P
                    last = nc.tensor.transpose(PP[m][:, j * P:(j + 1) * P], ADJ[:, c:c + P], ident[:, :])
                last.then_inc(adj_transposed, 1)

            def transpose_chunk(k, e, m):
                for j in range(CB):
                    c = (k[1]) * CH + j * P
                    last = nc.tensor.transpose(PP[m][:, j * P:(j + 1) * P], E[:, e, c:c + P], ident[:, :])
                last.then_inc(chunk_transposed, 1)

            def multiply(k, h, c):
                n = (2 * h + c) % 4
                acc = ACC[h % 2]
                pe.wait_ge(hi_ready, k + 1)
                for j in range(CB):
                    nc.tensor.matmul(acc[:, :], PT[:, n, 0, j * P:(j + 1) * P], H[:, c * CB + j, :],
                                     start=(c == 0 and j == 0), stop=False)
                pe.wait_ge(lo_ready, k + 1)
                for j in range(CB):
                    last = nc.tensor.matmul(acc[:, F:2 * F], PT[:, n, 1, j * P:(j + 1) * P],
                                            H[:, c * CB + j, 0:F], start=False, stop=(c == 1 and j == CB - 1))
                last.then_inc(chunk_multiplied, 1)

            def transpose_u(v):
                pe.wait_ge(u_ready, v + 1)
                for k in range(FK):
                    last = nc.tensor.transpose(PM[:, k * P:(k + 1) * P], U[:, k * P:(k + 1) * P], ident[:, :])
                last.then_inc(u_transposed, 1)

            def multiply_w(v, h):
                pe.wait_ge(ut_hi_ready, v + 1)
                for k in range(FK):
                    nc.tensor.matmul(PO[:, :], UT[:, 0, k * P:(k + 1) * P], W[:, k, h, :],
                                     start=(h == 0 and k == 0), stop=False)
                pe.wait_ge(ut_lo_ready, v + 1)
                for k in range(FK):
                    last = nc.tensor.matmul(PO[:, F:2 * F], UT[:, 1, k * P:(k + 1) * P], W[:, k, h, 0:F],
                                            start=False, stop=(h == HEADS - 1 and k == FK - 1))
                last.then_inc(w_multiplied, 1)

            def transpose_h1(b):
                pe.wait_ge(norm1_ready, b + 1)
                for k in range(FK):
                    last = nc.tensor.transpose(PM[:, k * P:(k + 1) * P], HN1[:, k * P:(k + 1) * P], ident[:, :])
                last.then_inc(h1_transposed, 1)

            def hidden(b):
                pe.wait_ge(h1_ready, b + 1)
                for k in range(FK):
                    last = nc.tensor.matmul(PM[:, 0:F], HT1[:, k, :], W1[:, k, :],
                                            start=(k == 0), stop=(k == FK - 1))
                last.then_inc(hid_summed, 1)

            def slot(ib, h):
                u = 4 * ib + h
                m0, m1 = chunk_buffers(h)
                if has(u + 1):
                    pe.wait_ge(probs_ready, u + 2)
                    pe.wait_ge(lo_ready, 2 * u + 2 if h in (0, 3) else 2 * u + 1)
                    transpose_chunk((u + 1, 0), (h + 1) % 2, m0)
                if not isinstance(u, int) or u >= 2:
                    pe.wait_ge(u_ready, u - 1)
                multiply(2 * u, h, 0)
                if has(u - 1):
                    if h == 0 and (not isinstance(ib, int) or ib >= 2):
                        pe.wait_ge(hid_ready, ib - 1)
                    elif h == 3 and (not isinstance(ib, int) or ib >= 1):
                        pe.wait_ge(h1_ready, ib)
                    elif not isinstance(u, int) or u > 1:
                        pe.wait_ge(ut_lo_ready, u - 1)
                    transpose_u(u - 1)
                if has(u + 1):
                    if h == 0:
                        pe.wait_ge(mask_ready, 2 * ib + 2)
                    elif h == 3:
                        pe.wait_ge(mask_ready, 2 * ib + 3)
                    else:
                        pe.wait_ge(lo_ready, 2 * u + 2)
                    transpose_chunk((u + 1, 1), (h + 1) % 2, m1)
                multiply(2 * u + 1, h, 1)
                if h >= 2 and not final(ib):
                    pe.wait_ge(lo_ready, 2 * u + 3)
                    adj_chunk(ib + 1, h - 2, h - 2)
                if has(u - 1):
                    if h == 1 and (not isinstance(ib, int) or ib >= 1):
                        pe.wait_ge(x1_ready, ib)
                    multiply_w(u - 1, (h - 1) % 4)
                if not isinstance(ib, int) or ib >= 1:
                    if h == 2:
                        transpose_h1(ib - 1)
                    if h == 3:
                        hidden(ib - 1)

            pe.wait_ge(d_ready, 2 * HEADS - 1)
            adj_chunk(0, 0, 0)
            pe.wait_ge(d_ready, 2 * HEADS)
            pe.wait_ge(probs_ready, 1)
            transpose_chunk((0, 0), 0, 1)
            pe.wait_ge(mask_ready, 1)
            transpose_chunk((0, 1), 0, 0)
            pe.wait_ge(lo_ready, 1)
            adj_chunk(0, 1, 1)

            pe.wait_ge(w_lo_ready, 1)
            pe.wait_ge(h_lo_ready, 4)
            pe.wait_ge(w1_in, 16)

            def body(ib):
                for h in range(HEADS):
                    slot(ib, h)
            block_loop(pe, body)
            pe.wait_ge(hid_ready, NB - 1)
            transpose_u(UNITS - 1)
            multiply_w(UNITS - 1, 3)
            transpose_h1(NB - 1)
            hidden(NB - 1)

            def aggregate(ib, j):
                pe.wait_ge(cast_ready, ib + 1)
                if not isinstance(ib, int) or ib >= 2:
                    pe.wait_ge(out_sum_ready, ib - 1)
                stat_t = PT[:, j, :, :].rearrange("p t (b c) -> p (t b) c", c=P)
                for b in range(NB):
                    if isinstance(ib, int) and ib == 0:
                        for n, (lo, _) in enumerate(HSPLIT):
                            if b == lo:
                                pe.wait_ge(hid_lo_ready, n + 1)
                        if b == NB - 1:
                            pe.wait_ge(hid_lo_ready, len(HSPLIT) + 1)
                    last = nc.tensor.matmul(ACC[j][:, :], stat_t[:, b, :], H[:, b, :],
                                            start=(b == 0), stop=(b == NB - 1))
                last.then_inc(out_summed, 1)
            pe.wait_ge(u_ready, UNITS)
            aggregate(0, 0)
            aggregate(1, 1)
            with pe.Fori(1, NB // 2) as pair:
                for j in range(2):
                    aggregate(2 * pair + j, j)

        @block.vector
        def _(vec):
            chain = [0]

            def link(ins):
                chain[0] += 1
                ins.then_inc(vec_step, 1)
                vec.wait_ge(vec_step, chain[0])

            for b in range(NB):
                if b % 4 == 0:
                    vec.wait_ge(x_in[b // 4], 16)
                last = nc.vector.bn_stats(ST[:, b, :], XA[:, b, :])
            link(last)
            me, qe, mo, qo = (ST[:, :, i] for i in (1, 2, 4, 5))
            nc.vector.tensor_tensor(LN[:, 0, :], me, mo, ALU.add)
            nc.vector.tensor_tensor(LN[:, 2, :], qe, qo, ALU.add)
            link(nc.vector.tensor_tensor(LN[:, 1, :], me, mo, ALU.subtract))
            nc.vector.tensor_tensor(LN[:, 3, :], LN[:, 1, :], LN[:, 1, :], ALU.mult)
            nc.vector.tensor_scalar(LN[:, 5, :], LN[:, 0, :], 0.5, None, ALU.mult)
            link(nc.vector.tensor_scalar(LN[:, 4, :], LN[:, 2, :], 1.0 / F, EPS, ALU.mult, ALU.add))
            nc.vector.scalar_tensor_tensor(LN[:, 6, :], LN[:, 3, :], 0.25, LN[:, 4, :], ALU.mult,
                                           ALU.add).then_inc(stats_ready, 1)
            vec.wait_ge(w0_in, 16)
            vec.wait_ge(a0_in, 16)
            for k in range(FK):
                for s in range(2):
                    for h in range(HEADS):
                        if k or s or h:
                            vec.wait_ge(vec_step, chain[0])
                        ins = nc.vector.tensor_tensor_reduce(
                            out=JUNK[:, :], in0=WR[:, k, h, :], in1=AB[:, h, s * F:(s + 1) * F], scale=1.0,
                            scalar=0.0, op0=ALU.mult, op1=ALU.add, accum_out=WA[:, k, s, h:h + 1])
                        chain[0] += 1
                        ins.then_inc(vec_step, 1)
            vec.wait_ge(vec_step, chain[0])
            vec.sem_inc(wa_ready, 1)
            vec.wait_ge(x_rstd_ready, 1)
            for b in range(NB):
                nc.vector.tensor_scalar(XA[:, b, :], XA[:, b, :], LN[:, 5, b:b + 1], LN[:, 7, b:b + 1],
                                        ALU.subtract, ALU.mult).then_inc(norm_ready, 1)
            for k in range(FK):
                last = nc.vector.tensor_copy(WDB[:, k, :, :], WA[:, k, 1, :].unsqueeze(2).to_broadcast([P, HEADS, P]))
            last.then_inc(wdb_ready, 1)
            for g in range(4):
                vec.wait_ge(h_hi_ready, g + 1)
                nc.vector.scalar_tensor_tensor(H[:, 4 * g:4 * g + 4, F:2 * F], XA[:, 4 * g:4 * g + 4, :], 0.0,
                                               H[:, 4 * g:4 * g + 4, 0:F], ALU.max, ALU.subtract).then_inc(h_lo_ready, 1)
            for k in range(FK):
                link(nc.vector.tensor_scalar(W[:, k, :, 0:F], WR[:, k, :, :], 1.0 / HEADS, None, ALU.mult))
                last = nc.vector.scalar_tensor_tensor(W[:, k, :, F:2 * F], WR[:, k, :, :], 1.0 / HEADS,
                                                      W[:, k, :, 0:F], ALU.mult, ALU.subtract)
            last.then_inc(w_lo_ready, 1)
            vec.wait_ge(b1_in, 16)

            def logits(u, h):
                vec.wait_ge(relu_ready, u + 1)
                vec.wait_ge(adj_dst_ready, u + 1)
                if not isinstance(u, int) or u >= HEADS:
                    vec.wait_ge(probs_ready, u - HEADS + 1)
                if not isinstance(u, int):
                    vec.sem_inc(passed_vec, 1)
                nc.vector.tensor_tensor_reduce(out=E[:, h % 2, :], in0=E[:, h % 2, :], in1=B[:, h % 2, :],
                                               scale=-1.0, scalar=3.0e38, op0=ALU.add, op1=ALU.min,
                                               accum_out=nmax[:, h:h + 1]).then_inc(logits_ready, 1)

            def low(k, n, m):
                vec.wait_ge(hi_ready, k + 1)
                nc.vector.tensor_tensor(PT[:, n, 1, :], PP[m][:, :], PT[:, n, 0, :], ALU.subtract)\
                    .then_inc(lo_ready, 1)

            def row_inverse(u, h):
                vec.wait_ge(probs_ready, u + 1)
                nc.vector.reciprocal(rinv[:, h:h + 1], rsum[:, h:h + 1]).then_inc(rinv_ready, 1)

            def u_sum(v, h):
                if not isinstance(v, int) or v >= 1:
                    vec.wait_ge(u_transposed, v)
                vec.wait_ge(half_ready, v + 1)
                nc.vector.scalar_tensor_tensor(U[:, :], ACC[h % 2][:, 0:F], rinv[:, h:h + 1], UH[:, :],
                                               ALU.mult, ALU.add).then_inc(u_ready, 1)

            def ut_low(v):
                vec.wait_ge(ut_hi_ready, v + 1)
                nc.vector.tensor_tensor(UT[:, 1, :], PM[:, 0:F], UT[:, 0, :], ALU.subtract).then_inc(ut_lo_ready, 1)

            def mask(ib, a, m):
                vec.wait_ge(adj_transposed, 2 * ib + a + 1)
                nc.vector.tensor_scalar(AT[:, a * CB:(a + 1) * CB, bass.ds(ib * P, P)],
                                        PP[m][:, :].rearrange("p (b c) -> p b c", c=P), 0.0, None,
                                        ALU.not_equal).then_inc(mask_ready, 1)

            def x1_block(b):
                vec.wait_ge(xres_in, 16 * (b + 1))
                vec.wait_ge(w_multiplied, 4 * b + 4)
                if not isinstance(b, int) or b >= 1:
                    vec.wait_ge(x1_stored, 16 * b)
                nc.vector.tensor_tensor(XS[:, :], PO[:, F:2 * F], XR[:, :], ALU.add).then_inc(x_sum_ready, 1)
                vec.wait_ge(x_sum_ready, b + 1)
                nc.vector.tensor_tensor(X1[:, :], PO[:, 0:F], XS[:, :], ALU.add).then_inc(x1_ready, 1)
                vec.wait_ge(x1_ready, b + 1)
                nc.vector.bn_stats(stat[:, :], X1[:, :]).then_inc(stat_ready, 1)
                vec.wait_ge(stat_ready, b + 1)
                if not isinstance(b, int):
                    vec.sem_inc(passed_vec, 1)
                nc.vector.bn_aggr(mv[:, :], stat[:, :]).then_inc(mv_ready, 1)
                vec.wait_ge(mv_ready, b + 1)
                nc.vector.tensor_scalar(veps[:, :], mv[:, 1:2], EPS, None, ALU.add).then_inc(veps_ready, 1)

            def norm1(b):
                vec.wait_ge(rstd_ready, b + 1)
                if not isinstance(b, int) or b >= 1:
                    vec.wait_ge(h1_transposed, b)
                nc.vector.tensor_scalar(HN1[:, :], X1[:, :], mv[:, 0:1], rstd[:, 0:1], ALU.subtract, ALU.mult)\
                    .then_inc(norm1_ready, 1)

            def hidden(b):
                if not isinstance(b, int) or b >= 1:
                    vec.wait_ge(hid_stored, 16 * b)
                vec.wait_ge(hid_summed, b + 1)
                nc.vector.tensor_tensor(HID[:, :], PM[:, 0:F], B1[:, :], ALU.add).then_inc(hid_ready, 1)

            def slot(ib, h):
                u = 4 * ib + h
                m0, m1 = chunk_buffers(h)
                if h == 0 and (not isinstance(ib, int) or ib >= 2):
                    hidden(ib - 2)
                if has(u + 2):
                    logits(u + 2, (h + 2) % 4)
                if has(u + 1):
                    low(2 * u + 2, (2 * h + 2) % 4, m0)
                if has(u - 1):
                    u_sum(u - 1, (h - 1) % 4)
                if h == 1 and (not isinstance(ib, int) or ib >= 1):
                    x1_block(ib - 1)
                if has(u - 1):
                    ut_low(u - 1)
                if h == 2 and (not isinstance(ib, int) or ib >= 1):
                    norm1(ib - 1)
                if has(u + 1):
                    low(2 * u + 3, (2 * h + 3) % 4, m1)
                row_inverse(u, h)
                if h >= 2 and not final(ib):
                    mask(ib + 1, h - 2, h - 2)

            logits(0, 0)
            mask(0, 0, 0)
            logits(1, 1)
            low(0, 0, 1)
            low(1, 1, 0)
            mask(0, 1, 1)

            def body(ib):
                for h in range(HEADS):
                    slot(ib, h)
            block_loop(vec, body, first=3)
            hidden(NB - 2)
            u_sum(UNITS - 1, 3)
            ut_low(UNITS - 1)
            x1_block(NB - 1)
            norm1(NB - 1)

            def degree(ib):
                nc.vector.tensor_reduce(deg[:, bass.ds(ib, 1)], AT[:, bass.ds(ib, 1), :], mybir.AxisListType.XY,
                                        ALU.add).then_inc(deg_ready, 1)
                vec.wait_ge(deg_ready, ib + 1)
                if not isinstance(ib, int):
                    vec.sem_inc(passed_vec, 1)
                nc.vector.reciprocal(rdeg[:, bass.ds(ib, 1)], deg[:, bass.ds(ib, 1)]).then_inc(rdeg_ready, 1)

            vec.wait_ge(hid_in, 16)
            for n, (lo, hi) in enumerate(HSPLIT):
                vec.wait_ge(hid_hi_ready, n + 1)
                nc.vector.tensor_tensor(H[:, lo:hi, F:2 * F], HIN[:, lo:hi, :], H[:, lo:hi, 0:F],
                                        ALU.subtract).then_inc(hid_lo_ready, 1)
            hidden(NB - 1)
            vec.wait_ge(hid_hi_ready, len(HSPLIT) + 1)
            nc.vector.tensor_tensor(H[:, NB - 1, F:2 * F], HID[:, :], H[:, NB - 1, 0:F],
                                    ALU.subtract).then_inc(hid_lo_ready, 1)
            degree(0)
            vec.wait_ge(x1_in, 16)

            def finish(ib, j):
                if not isinstance(ib, int) or ib >= 2:
                    vec.wait_ge(out_stored[j], 8 * (ib - j))
                vec.wait_ge(out_half_ready, ib + 1)
                if not isinstance(ib, int):
                    vec.sem_inc(passed_vec, 1)
                nc.vector.scalar_tensor_tensor(OS[:, j, :], ACC[j][:, 0:F], rdeg[:, bass.ds(ib, 1)], OH[:, j, :],
                                               ALU.mult, ALU.add).then_inc(out_sum_ready, 1)
                vec.wait_ge(out_sum_ready, ib + 1)
                if not isinstance(ib, int):
                    vec.sem_inc(passed_vec, 1)
                nc.vector.tensor_tensor(OUT[:, j, :], OS[:, j, :], X1R[:, bass.ds(ib, 1), :].rearrange("p b f -> p (b f)"),
                                        ALU.add).then_inc(out_ready, 1)

            degree(1)
            finish(0, 0)
            degree(2)
            finish(1, 1)
            with vec.Fori(1, NB // 2 - 1) as pair:
                for j in range(2):
                    degree(2 * pair + j + 1)
                    finish(2 * pair + j, j)
            degree(NB - 1)
            finish(NB - 2, 0)
            finish(NB - 1, 1)


def chunk_buffers(h):
    return (1, 0) if h == 3 else (0, 1)


_INS = ["x", "adj", "L0_gnn_W", "L0_gnn_a", "L1_gnn_W", "L1_gnn_b"]


def kernel(**inputs):
    import numpy as np
    import concourse.bacc as bacc
    from concourse.bass_utils import run_bass_kernel_spmd

    nc = bacc.Bacc("TRN2", target_bir_lowering=False, num_devices=1)
    arrays, args = {}, []
    for name in _INS:
        a = np.ascontiguousarray(inputs[name])
        arrays["in_" + name] = a
        args.append(nc.dram_tensor("in_" + name, a.shape, mybir.dt.from_np(a.dtype), kind="ExternalInput").ap())
    out = nc.dram_tensor("out_0", (N, F), mybir.dt.float32, kind="ExternalOutput").ap()
    gnn_kernel(nc, *args, out)
    return run_bass_kernel_spmd(nc, [arrays], core_ids=[0]).results[0]["out_0"]
```

```python
from contextlib import ExitStack

import concourse.bass as bass
from concourse import mybir

P = 128
N = 2048
F = 256
HEADS = 4
NB = N // P
FK = F // P
UNITS = NB * HEADS
SLOPE = 0.01
EPS = 1e-5
P_SCALE = 2.0 ** 15
H_SCALE = 2.0 ** 11
W_SCALE = 1.0 / (HEADS * P_SCALE * H_SCALE)


def gnn_kernel(nc, x, adj, w0, a0, w1, b1, out):
    fp32 = mybir.dt.float32
    f32r = mybir.dt.float32r
    fp16 = mybir.dt.float16
    bf16 = mybir.dt.bfloat16
    u8 = mybir.dt.uint8
    ALU = mybir.AluOpType
    ACT = mybir.ActivationFunctionType

    x1_dram = nc.dram_tensor("x1_scratch", (N, F), fp32, kind="Internal").ap()
    hid_dram = nc.dram_tensor("hidden_scratch", (N, F), fp32, kind="Internal").ap()
    dst_dram = nc.dram_tensor("dst_scratch", (HEADS, NB, P), fp32, kind="Internal").ap()

    def blocks(t):
        return t.rearrange("(b p) f -> p b f", p=P)

    ctx = ExitStack()
    with ctx:
        where = {"": (nc.sbuf_base + 63) // 64 * 64}

        def size(shape, dt):
            n = 1
            for s in shape[1:]:
                n *= s
            return n * {fp32: 4, f32r: 4, fp16: 2, bf16: 2, u8: 1}[dt]

        def place(name, shape, dt):
            at = where[""]
            where[name] = at
            where[""] = at + (size(shape, dt) + 31) // 32 * 32
            assert where[""] <= nc.sbuf_usable_end, name
            return nc.alloc_sbuf_tensor_at(name, shape, dt, offset=at)

        def alias(name, shape, dt, over, skip=0):
            return nc.alloc_sbuf_tensor_at(name, shape, dt, offset=where[over] + skip)

        D = place("dst_rows", [P, HEADS, N], fp32)
        AT = place("mask_t", [P, NB, N], u8)
        H = place("h_split", [P, NB, 2 * F], fp16)
        W = place("w0_split", [P, FK, HEADS, 2 * F], f32r)
        E = place("logits", [P, HEADS, N], fp32)
        B = place("adj_dst", [P, 2, N], fp32)
        ADJ = place("adj_rows", [P, N], fp32)
        MR = place("mask_rows", [P, N], bf16)
        MT = place("mask_cols", [P, NB, P], bf16)
        PA = place("probs_hi", [P, 2, N], fp16)
        PB = place("probs_lo", [P, 2, N], fp16)
        TA = place("probs_hi_t", [P, 2, NB, P], fp16)
        TB = place("probs_lo_t", [P, 2, NB, P], fp16)
        U = place("u_rows", [P, F], fp32)
        UH = place("u_half", [P, F], fp32)
        UT = place("u_t", [P, 2, F], f32r)
        W1 = place("w1", [P, FK, F], fp32)
        B1 = place("b1_rows", [P, F], fp32)
        XR = place("x_res", [P, F], fp32)
        XS = place("x_sum", [P, F], fp32)
        X1 = place("x1", [P, F], fp32)
        HN1 = place("x1_norm", [P, F], fp32)
        HT1 = place("h1_t", [P, FK, P], fp32)
        HID = place("hidden", [P, F], fp32)
        ident = place("ident", [P, P], fp32)
        src = place("src_bias", [P, UNITS], fp32)
        nmax = place("neg_max", [P, HEADS], fp32)
        rsum = place("row_sum", [P, HEADS], fp32)
        rinv = place("row_inv", [P, HEADS], fp32)
        stat = place("stat", [P, 6], fp32)
        mv = place("mean_var", [P, 2], fp32)
        veps = place("var_eps", [P, 1], fp32)
        rstd = place("rstd", [P, 1], fp32)
        power = place("power", [P, NB], fp32)
        deg = place("deg", [P, NB], fp32)
        rdeg = place("rdeg", [P, NB], fp32)

        XA = alias("x_all", [P, NB, F], fp32, "logits", 4 * 2 * N)
        WR = alias("w0_raw", [P, FK, HEADS, F], fp32, "adj_dst")
        AB = alias("a_rows", [P, HEADS, 2 * F], fp32, "adj_dst", 4 * N)
        HT = alias("h_t", [P, FK, N], fp32, "probs_hi_t")
        o = 0
        WA = alias("wa", [P, FK, 2, HEADS], fp32, "probs_lo", o)
        o += 4 * FK * 2 * HEADS
        JUNK = alias("junk", [P, F], fp32, "probs_lo", o)
        o += 4 * F
        ST = alias("x_stats", [P, NB, 6], fp32, "probs_lo", o)
        o += 4 * NB * 6
        MV = alias("x_mean_var", [P, NB, 2], fp32, "probs_lo", o)
        o += 4 * NB * 2
        VE = alias("x_var_eps", [P, NB], fp32, "probs_lo", o)
        o += 4 * NB
        RS = alias("x_rstd", [P, NB], fp32, "probs_lo", o)
        o += 4 * NB
        MB = alias("x_bias", [P, NB], fp32, "probs_lo", o)
        o += 4 * NB
        DC = alias("dst_cols", [P, HEADS, NB], fp32, "probs_lo", o)
        o += 4 * NB * HEADS
        DR = alias("dst_block_rows", [NB * HEADS, P], fp32, "probs_lo", o)
        HIN = alias("hidden_in", [P, NB, F], fp32, "adj_dst")
        HS = alias("hidden_split", [P, NB, 2 * F], f32r, "logits")
        X1R = alias("x1_in", [P, NB, F], fp32, "h_split")
        MC = alias("mask_columns", [P, 2, NB, P], f32r, "probs_hi")
        OH = alias("out_half", [P, 2, F], fp32, "adj_rows")
        OS = alias("out_sum", [P, 2, F], fp32, "adj_rows", 8 * F)
        OUT = alias("out_rows", [P, 2, F], fp32, "adj_rows", 16 * F)

        def psum(name, cols):
            return ctx.enter_context(nc.psum_tensor(name, [P, cols], fp32))

        PP = [psum(f"ps_pair{i}", 4 * F) for i in range(2)]
        PU = [t[:, 0:F] for t in PP]
        PH, PG = PP[0][:, 2 * F:3 * F], PP[1][:, 2 * F:3 * F]
        ACC = [psum(f"ps_acc{i}", 2 * F) for i in range(2)]
        PO = psum("ps_out", 2 * F)
        PM = psum("ps_misc", 2 * F)

        def sem(name):
            return ctx.enter_context(nc.semaphore(name))

        x_in = [sem(f"x_in{g}") for g in range(4)]
        w0_in, a0_in, w1_in, b1_in = sem("w0_in"), sem("a0_in"), sem("w1_in"), sem("b1_in")
        adj_in, xres_in = sem("adj_in"), sem("xres_in")
        x1_stored, hid_stored = sem("x1_stored"), sem("hid_stored")
        hid_in, x1_in, out_stored = sem("hid_in"), sem("x1_in"), [sem("out_stored0"), sem("out_stored1")]
        dst_stored, dst_in = sem("dst_stored"), [sem(f"dst_in{h}") for h in range(HEADS)]
        zeroed, ident_ready, power_ready = sem("zeroed"), sem("ident_ready"), sem("power_ready")
        vec_step = sem("vec_step")
        x_var_ready, x_rstd_ready, x_bias_ready = sem("x_var_ready"), sem("x_rstd_ready"), sem("x_bias_ready")
        h_ready, h_hi_ready, h_lo_ready = sem("h_ready"), sem("h_hi_ready"), sem("h_lo_ready")
        h_transposed, ht_ready = sem("h_transposed"), sem("ht_ready")
        wa_ready, w_hi_ready, w_lo_ready = sem("wa_ready"), sem("w_hi_ready"), sem("w_lo_ready")
        sd_summed, src_ready, dst_cols_ready = sem("sd_summed"), sem("src_ready"), sem("dst_cols_ready")
        dst_transposed, dst_rows_ready = sem("dst_transposed"), sem("dst_rows_ready")
        adj_dst0_ready = sem("adj_dst0_ready")
        adj_dst_ready = sem("adj_dst_ready")
        relu_ready = sem("relu_ready")
        logits_ready = sem("logits_ready")
        probs_ready = sem("probs_ready")
        rinv_ready = sem("rinv_ready")
        probs_hi_ready, probs_lo_ready = sem("probs_hi_ready"), sem("probs_lo_ready")
        hi_in = [sem("hi_in0"), sem("hi_in1")]
        lo_in = [sem("lo_in0"), sem("lo_in1")]
        hi_multiplied, unit_multiplied = sem("hi_multiplied"), sem("unit_multiplied")
        half_ready, u_ready = sem("half_ready"), sem("u_ready")
        u_transposed, ut_hi_ready, ut_lo_ready = sem("u_transposed"), sem("ut_hi_ready"), sem("ut_lo_ready")
        w_multiplied = sem("w_multiplied")
        mask_rows_ready = sem("mask_rows_ready")
        mask_in, mask_ready = sem("mask_in"), sem("mask_ready")
        x_sum_ready, x1_ready, stat_ready, mv_ready, veps_ready, rstd_ready = (
            sem("x_sum_ready"), sem("x1_ready"), sem("stat_ready"), sem("mv_ready"),
            sem("veps_ready"), sem("rstd_ready"))
        norm1_ready, h1_transposed, h1_ready, hid_summed, hid_ready = (
            sem("norm1_ready"), sem("h1_transposed"), sem("h1_ready"), sem("hid_summed"),
            sem("hid_ready"))
        hid_hi_ready, hid_lo_ready = sem("hid_hi_ready"), sem("hid_lo_ready")
        cast_ready, out_summed, out_half_ready = sem("cast_ready"), sem("out_summed"), sem("out_half_ready")
        deg_ready, rdeg_ready, out_sum_ready, out_ready = (
            sem("deg_ready"), sem("rdeg_ready"), sem("out_sum_ready"), sem("out_ready"))
        passed_vec, passed_act, passed_pool, passed_sp = (
            sem("passed_vec"), sem("passed_act"), sem("passed_pool"), sem("passed_sp"))

        HALF = NB // 2
        BACK = NB - 2
        EARLY = BACK - 1

        def has(u):
            return not isinstance(u, int) or 0 <= u < UNITS

        def block_loop(eng, body, first=3):
            for ib in range(first):
                body(ib)
            with eng.Fori(first, NB - 1) as ib:
                body(ib)
            body(NB - 1)

        def final(ib):
            return isinstance(ib, int) and ib == NB - 1

        block = ctx.enter_context(nc.Block())

        @block.sync
        def _(sp):
            for g in range(4):
                sp.dma_start(XA[:, 4 * g:4 * g + 4, :], blocks(x)[:, 4 * g:4 * g + 4, :]).then_inc(x_in[g], 16)
            sp.dma_start(AB[:, :, :].rearrange("p h d -> p (h d)"), a0.rearrange("h d o -> (h d o)").partition_broadcast(P)).then_inc(a0_in, 16)
            sp.dma_start(WR[:, :, :, :], w0.rearrange("(k p) (h d) -> p k h d", p=P, h=HEADS)).then_inc(w0_in, 16)
            sp.dma_start(ADJ[:, :], adj[0:P, :]).then_inc(adj_in, 16)
            sp.dma_start(W1[:, :, :], w1.rearrange("(k p) f -> p k f", p=P)).then_inc(w1_in, 16)
            sp.dma_start(B1[:, :], b1.partition_broadcast(P)).then_inc(b1_in, 16)

            sp.wait_ge(dst_rows_ready, 1)
            for h in range(HEADS):
                sp.dma_start(dst_dram[h, :, :], DR[h * NB:(h + 1) * NB, :]).then_inc(dst_stored, 16)
            sp.wait_ge(dst_stored, 16 * HEADS)
            for h in range(HEADS):
                sp.dma_start(D[:, h, :], dst_dram[h, :, :].rearrange("b p -> (b p)").partition_broadcast(P))\
                    .then_inc(dst_in[h], 16)

            def passed(b):
                if not isinstance(b, int):
                    sp.sem_inc(passed_sp, 1)

            def store_hidden(b):
                sp.wait_ge(hid_ready, b + 1)
                passed(b)
                sp.dma_start(hid_dram[bass.ds(b * P, P), :], HID[:, :]).then_inc(hid_stored, 16)

            def store_x1(b):
                sp.wait_ge(x1_ready, b + 1)
                passed(b)
                sp.dma_start(x1_dram[bass.ds(b * P, P), :], X1[:, :]).then_inc(x1_stored, 16)

            def load_adj(ib):
                sp.wait_ge(adj_dst_ready, 4 * ib - 1)
                passed(ib)
                sp.wait_ge(mask_rows_ready, ib)
                passed(ib)
                sp.dma_start(ADJ[:, :], adj[bass.ds(ib * P, P), :]).then_inc(adj_in, 16)

            def transpose_hi(u, e):
                sp.wait_ge(probs_hi_ready, u + 1)
                passed(u)
                if not isinstance(u, int) or u >= 2:
                    sp.wait_ge(hi_multiplied, u - 1)
                    passed(u)
                sp.dma_start_transpose(TA[:, e, :, :], PA[:, e, :]).then_inc(hi_in[e], 16)

            def transpose_lo(u, e):
                sp.wait_ge(probs_lo_ready, u + 1)
                passed(u)
                if not isinstance(u, int) or u >= 2:
                    sp.wait_ge(unit_multiplied, u - 1)
                    passed(u)
                sp.dma_start_transpose(TB[:, e, :, :], PB[:, e, :]).then_inc(lo_in[e], 16)

            def transpose_mask(b):
                sp.wait_ge(mask_rows_ready, b + 1)
                passed(b)
                if not isinstance(b, int) or b >= 1:
                    sp.wait_ge(mask_ready, b)
                    passed(b)
                sp.dma_start_transpose(MT[:, :, :], MR[:, :]).then_inc(mask_in, 16)

            def slot(ib, h):
                u = 4 * ib + h
                if h == 3 and not (isinstance(ib, int) and ib + 2 >= NB):
                    load_adj(ib + 2)
                if has(u + 2):
                    transpose_hi(u + 2, h % 2)
                if h == 2 and not final(ib):
                    transpose_mask(ib + 1)
                if h == 3:
                    if not isinstance(ib, int) or ib >= 2:
                        store_hidden(ib - 2)
                    if not isinstance(ib, int) or ib >= 1:
                        store_x1(ib - 1)
                    sp.dma_start(XR[:, :], x[bass.ds(ib * P, P), :]).then_inc(xres_in, 16)
                if has(u + 2):
                    transpose_lo(u + 2, h % 2)
                if final(ib) and h == 1:
                    sp.wait_ge(hid_stored, 16 * EARLY)
                    sp.wait_ge(logits_ready, UNITS)
                    sp.dma_start(HIN[:, 0:EARLY, :], blocks(hid_dram)[:, 0:EARLY, :]).then_inc(hid_in, 16)

            for u in range(2):
                transpose_hi(u, u)
                transpose_lo(u, u)
            transpose_mask(0)
            load_adj(1)

            def body(ib):
                for h in range(HEADS):
                    slot(ib, h)
            for ib in range(3):
                body(ib)
            with sp.Fori(3, NB - 2) as ib:
                body(ib)
            body(NB - 2)
            body(NB - 1)
            sp.wait_ge(hid_stored, 16 * BACK)
            sp.dma_start(HIN[:, EARLY:BACK, :], blocks(hid_dram)[:, EARLY:BACK, :]).then_inc(hid_in, 16)
            sp.wait_ge(x1_stored, 16 * (NB - 1))
            sp.wait_ge(unit_multiplied, UNITS)
            sp.dma_start(X1R[:, 0:NB - 1, :], blocks(x1_dram)[:, 0:NB - 1, :]).then_inc(x1_in, 16)

            def store(ib, j):
                sp.wait_ge(out_ready, ib + 1)
                passed(ib)
                sp.dma_start(out[bass.ds(ib * P, P), :], OUT[:, j, :]).then_inc(out_stored[j], 16)
            with sp.Fori(0, NB // 2) as pair:
                for j in range(2):
                    store(2 * pair + j, j)
            for j in range(2):
                sp.wait_ge(out_stored[j], 8 * NB)

        @block.gpsimd
        def _(pool):
            nc.gpsimd.memset(ident[:, :], 0.0).then_inc(zeroed, 1)
            nc.gpsimd.memset(power[:, :], -0.5).then_inc(power_ready, 1)
            pool.wait_ge(zeroed, 1)
            nc.gpsimd.affine_select(out=ident[:, :], in_=ident[:, :], compare_op=ALU.not_equal, fill=1.0,
                                    base=0, pattern=[[-1, P]], channel_multiplier=1).then_inc(ident_ready, 1)
            pool.wait_ge(power_ready, 1)
            for g in range(4):
                c = slice(4 * g, 4 * g + 4)
                pool.wait_ge(x_var_ready, g + 1)
                nc.gpsimd.tensor_tensor(RS[:, c], VE[:, c], power[:, c], ALU.pow).then_inc(x_rstd_ready, 1)

            def adj_dst(ib, h):
                u = 4 * ib + h
                if h == 0:
                    pool.wait_ge(adj_in, 16 * (ib + 1))
                if isinstance(u, int) and u < HEADS:
                    pool.wait_ge(dst_in[h], 16)
                if not isinstance(u, int) or u >= 2:
                    pool.wait_ge(logits_ready, u - 1)
                    pool.sem_inc(passed_pool, 1)
                elif u == 1:
                    pool.wait_ge(adj_in, 16)
                    pool.wait_ge(wa_ready, 1)
                nc.gpsimd.tensor_tensor(B[:, h % 2, :], ADJ[:, :], D[:, h, :], ALU.add).then_inc(adj_dst_ready, 1)

            def rstd_of(b):
                pool.wait_ge(veps_ready, b + 1)
                pool.sem_inc(passed_pool, 1)
                nc.gpsimd.tensor_tensor(rstd[:, :], veps[:, :], power[:, 0:1], ALU.pow).then_inc(rstd_ready, 1)

            def body(ib):
                for h in range(HEADS):
                    if not isinstance(ib, int) or ib + h >= 1:
                        adj_dst(ib, h)
                    if h == 2 and (not isinstance(ib, int) or ib >= 2):
                        rstd_of(ib - 2)
            block_loop(pool, body)
            rstd_of(NB - 2)
            rstd_of(NB - 1)

        @block.scalar
        def _(act):
            for g in range(4):
                act.wait_ge(x_bias_ready, g + 1)
                for b in range(4 * g, 4 * g + 4):
                    last = nc.scalar.activation(XA[:, b, :], XA[:, b, :], ACT.Relu, scale=RS[:, b:b + 1],
                                                bias=MB[:, b:b + 1])
                last.then_inc(h_ready, 1)
            for g in range(4):
                act.wait_ge(h_transposed, g + 1)
                nc.scalar.activation(
                    HT[:, :, 4 * g * P:(4 * g + 4) * P].rearrange("p k (b c) -> p b k c", b=4),
                    PP[g % 2][:, :].rearrange("p (b k c) -> p b k c", b=4, k=FK),
                    ACT.Copy).then_inc(ht_ready, 1)
            for g in range(4):
                nc.scalar.activation(H[:, 4 * g:4 * g + 4, 0:F], XA[:, 4 * g:4 * g + 4, :],
                                     ACT.Copy, scale=H_SCALE).then_inc(h_hi_ready, 1)
            act.wait_ge(sd_summed, 1)
            sd = PM[:, 0:NB * 2 * HEADS].rearrange("p (b s h) -> p b s h", s=2, h=HEADS)
            nc.scalar.activation(DC[:, :, :].rearrange("p h b -> p b h"), sd[:, :, 1, :], ACT.Copy).then_inc(dst_cols_ready, 1)
            nc.scalar.activation(src[:, :].rearrange("p (b h) -> p b h", h=HEADS), sd[:, :, 0, :], ACT.Copy,
                                 scale=-(1.0 - SLOPE)).then_inc(src_ready, 1)
            act.wait_ge(dst_transposed, 1)
            nc.scalar.activation(DR[:, :], ACC[0][0:NB * HEADS, 0:P], ACT.Copy).then_inc(dst_rows_ready, 1)

            def relu_term(u, h):
                if isinstance(u, int) and u < HEADS:
                    if u == 0:
                        act.wait_ge(src_ready, 1)
                    if u == 2:
                        act.wait_ge(h_hi_ready, 4)
                        act.wait_ge(h_lo_ready, 4)
                else:
                    act.wait_ge(probs_lo_ready, u - HEADS + 1)
                if isinstance(u, int) and u < HEADS:
                    act.wait_ge(dst_in[u], 16)
                if not isinstance(u, int):
                    act.sem_inc(passed_act, 1)
                nc.scalar.activation(E[:, h, :], D[:, h, :], ACT.Relu, scale=-(1.0 - SLOPE),
                                     bias=src[:, bass.ds(u, 1)]).then_inc(relu_ready, 1)

            def exp(u, h):
                act.wait_ge(logits_ready, u + 1)
                if not isinstance(u, int) or u >= HEADS:
                    act.wait_ge(rinv_ready, u - HEADS + 1)
                nc.scalar.activation(E[:, h, :], E[:, h, :], ACT.Exp, scale=-1.0,
                                     bias=nmax[:, h:h + 1], accum_out=rsum[:, h:h + 1]).then_inc(probs_ready, 1)

            def high(v, k, h):
                act.wait_ge(probs_ready, v + 1)
                if not isinstance(v, int) or v >= 2:
                    act.wait_ge(hi_in[h % 2], 16 * k)
                nc.scalar.activation(PA[:, h % 2, :], E[:, h, :], ACT.Copy, scale=P_SCALE)\
                    .then_inc(probs_hi_ready, 1)

            def u_half(v, h):
                act.wait_ge(rinv_ready, v + 1)
                if not isinstance(v, int) or v >= 1:
                    act.wait_ge(u_ready, v)
                act.wait_ge(unit_multiplied, v + 1)
                nc.scalar.activation(UH[:, :], ACC[h % 2][:, F:2 * F], ACT.Copy,
                                     scale=rinv[:, h:h + 1]).then_inc(half_ready, 1)

            def ut_high(v, h):
                if not isinstance(v, int) or v >= 1:
                    act.wait_ge(w_multiplied, v)
                act.wait_ge(u_transposed, v + 1)
                nc.scalar.activation(UT[:, 0, :], PU[h % 2], ACT.Copy).then_inc(ut_hi_ready, 1)

            def h1_relu(b):
                if not isinstance(b, int) or b >= 1:
                    act.wait_ge(hid_summed, b)
                act.wait_ge(h1_transposed, b + 1)
                nc.scalar.activation(HT1[:, :, :], PH.rearrange("p (k c) -> p k c", k=FK),
                                     ACT.Relu).then_inc(h1_ready, 1)

            def slot(ib, h):
                u = 4 * ib + h
                if has(u - 2):
                    ut_high(u - 2, (h - 2) % 4)
                if has(u - 1):
                    u_half(u - 1, (h - 1) % 4)
                if has(u + 2):
                    high(u + 2, 2 * ib + (h + 2) // 2, (h + 2) % 4)
                if h == 0 and (not isinstance(ib, int) or ib >= 2):
                    h1_relu(ib - 2)
                if has(u + 3):
                    exp(u + 3, (h + 3) % 4)
                if has(u + 4):
                    relu_term(u + 4, h)
                if final(ib) and h == 2:
                    cast(0, 0)
                if final(ib) and h == 3:
                    act.wait_ge(hid_in, 16)
                    act.wait_ge(probs_lo_ready, UNITS)
                    hidden_high(0, EARLY, HIN[:, 0:EARLY, :])

            def cast(ib, j):
                if not isinstance(ib, int) or ib >= 2:
                    act.wait_ge(out_summed, ib - 1)
                    act.sem_inc(passed_act, 1)
                else:
                    act.wait_ge(mask_ready, NB)
                    act.wait_ge(probs_lo_ready, UNITS)
                    for e in range(2):
                        act.wait_ge((hi_in, lo_in)[ib][e], 16 * UNITS // 2)
                nc.scalar.activation(MC[:, j, :, :], AT[:, :, bass.ds(ib * P, P)], ACT.Copy).then_inc(cast_ready, 1)

            def hidden_high(lo, hi, rows):
                nc.scalar.activation(HS[:, lo:hi, 0:F], rows, ACT.Copy).then_inc(hid_hi_ready, 1)

            relu_term(0, 0)
            relu_term(1, 1)
            exp(0, 0)
            high(0, 0, 0)
            relu_term(2, 2)
            exp(1, 1)
            high(1, 0, 1)
            exp(2, 2)
            relu_term(3, 3)

            def body(ib):
                for h in range(HEADS):
                    slot(ib, h)
            block_loop(act, body)
            ut_high(UNITS - 2, 2)
            h1_relu(NB - 2)
            u_half(UNITS - 1, 3)
            act.wait_ge(hid_in, 32)
            hidden_high(EARLY, BACK, HIN[:, EARLY:BACK, :])
            cast(1, 1)
            act.wait_ge(hid_ready, NB - 1)
            hidden_high(NB - 2, NB - 1, HID[:, :].rearrange("p (b f) -> p b f", b=1))
            ut_high(UNITS - 1, 3)
            h1_relu(NB - 1)
            act.wait_ge(hid_ready, NB)
            hidden_high(NB - 1, NB, HID[:, :].rearrange("p (b f) -> p b f", b=1))

            def out_half(ib, j):
                act.wait_ge(rdeg_ready, ib + 1)
                if not isinstance(ib, int) or ib >= 2:
                    act.wait_ge(out_sum_ready, ib - 1)
                act.wait_ge(out_summed, ib + 1)
                if not isinstance(ib, int):
                    act.sem_inc(passed_act, 1)
                nc.scalar.activation(OH[:, j, :], ACC[j][:, F:2 * F], ACT.Copy,
                                     scale=rdeg[:, bass.ds(ib, 1)]).then_inc(out_half_ready, 1)
            out_half(0, 0)
            cast(2, 0)
            out_half(1, 1)
            cast(3, 1)
            with act.Fori(1, NB // 2 - 1) as pair:
                for j in range(2):
                    out_half(2 * pair + j, j)
                    cast(2 * pair + j + 2, j)
            for j in range(2):
                out_half(NB - 2 + j, j)

        @block.tensor
        def _(pe):
            pe.wait_ge(ident_ready, 1)
            for g in range(4):
                pe.wait_ge(h_ready, g + 1)
                if g >= 2:
                    pe.wait_ge(ht_ready, g - 1)
                for b in range(4):
                    for k in range(FK):
                        c = (b * FK + k) * P
                        last = nc.tensor.transpose(PP[g % 2][:, c:c + P], XA[:, 4 * g + b, k * P:(k + 1) * P],
                                                   ident[:, :])
                last.then_inc(h_transposed, 1)
            pe.wait_ge(wa_ready, 1)
            for b in range(NB):
                if b % 4 == 0:
                    pe.wait_ge(ht_ready, b // 4 + 1)
                for k in range(FK):
                    c = b * 2 * HEADS
                    last = nc.tensor.matmul(PM[:, c:c + 2 * HEADS], HT[:, k, b * P:(b + 1) * P], WA[:, k, :, :],
                                            start=(k == 0), stop=(k == FK - 1))
            last.then_inc(sd_summed, 1)
            pe.wait_ge(dst_cols_ready, 1)
            nc.tensor.transpose(ACC[0][0:NB * HEADS, 0:P], DC[:, :, :].rearrange("p h b -> p (h b)"),
                                ident[:, :]).then_inc(dst_transposed, 1)

            def multiply(u, k, h):
                e = h % 2
                pe.wait_ge(hi_in[e], 16 * (k + 1))
                if not isinstance(u, int) or u >= 2:
                    pe.wait_ge(u_ready, u - 1)
                for b in range(NB):
                    last = nc.tensor.matmul(ACC[e][:, :], TA[:, e, b, :], H[:, b, :], start=(b == 0), stop=False)
                last.then_inc(hi_multiplied, 1)

            def multiply_low(k, h):
                e = h % 2
                pe.wait_ge(lo_in[e], 16 * (k + 1))
                for b in range(NB):
                    last = nc.tensor.matmul(ACC[e][:, F:2 * F], TB[:, e, b, :], H[:, b, 0:F],
                                            start=False, stop=(b == NB - 1))
                last.then_inc(unit_multiplied, 1)

            def transpose_u(v, h):
                pe.wait_ge(u_ready, v + 1)
                for k in range(FK):
                    last = nc.tensor.transpose(PU[h % 2][:, k * P:(k + 1) * P], U[:, k * P:(k + 1) * P], ident[:, :])
                last.then_inc(u_transposed, 1)

            def multiply_w(v, h):
                pe.wait_ge(ut_hi_ready, v + 1)
                for k in range(FK):
                    nc.tensor.matmul(PO[:, :], UT[:, 0, k * P:(k + 1) * P], W[:, k, h, :],
                                     start=(h == 0 and k == 0), stop=False)
                pe.wait_ge(ut_lo_ready, v + 1)
                for k in range(FK):
                    last = nc.tensor.matmul(PO[:, F:2 * F], UT[:, 1, k * P:(k + 1) * P], W[:, k, h, 0:F],
                                            start=False, stop=(h == HEADS - 1 and k == FK - 1))
                last.then_inc(w_multiplied, 1)

            def transpose_h1(b):
                pe.wait_ge(norm1_ready, b + 1)
                if not isinstance(b, int) or b >= 1:
                    pe.wait_ge(h1_ready, b)
                for k in range(FK):
                    last = nc.tensor.transpose(PH[:, k * P:(k + 1) * P], HN1[:, k * P:(k + 1) * P], ident[:, :])
                last.then_inc(h1_transposed, 1)

            def hidden(b):
                pe.wait_ge(h1_ready, b + 1)
                if not isinstance(b, int) or b >= 1:
                    pe.wait_ge(hid_ready, b)
                for k in range(FK):
                    last = nc.tensor.matmul(PG, HT1[:, k, :], W1[:, k, :],
                                            start=(k == 0), stop=(k == FK - 1))
                last.then_inc(hid_summed, 1)

            def slot(ib, h):
                u = 4 * ib + h
                multiply(u, 2 * ib + h // 2, h)
                if has(u - 2):
                    if h == 2 and (not isinstance(ib, int) or ib >= 1):
                        pe.wait_ge(x1_ready, ib)
                    multiply_w(u - 2, (h - 2) % 4)
                if h == 1 and (not isinstance(ib, int) or ib >= 2):
                    hidden(ib - 2)
                multiply_low(2 * ib + h // 2, h)
                if h == 3 and (not isinstance(ib, int) or ib >= 1):
                    transpose_h1(ib - 1)
                if has(u - 1):
                    transpose_u(u - 1, (h - 1) % 4)

            pe.wait_ge(w_lo_ready, 1)
            pe.wait_ge(h_lo_ready, 4)
            pe.wait_ge(w1_in, 16)

            def body(ib):
                for h in range(HEADS):
                    slot(ib, h)
            block_loop(pe, body)

            def aggregate(ib, j, lo=0, hi=NB):
                if lo == 0:
                    pe.wait_ge(cast_ready, ib + 1)
                    if not isinstance(ib, int) or ib >= 2:
                        pe.wait_ge(out_sum_ready, ib - 1)
                for b in range(lo, hi):
                    last = nc.tensor.matmul(ACC[j][:, :], MC[:, j, b, :], HS[:, b, :],
                                            start=(b == 0), stop=(b == NB - 1))
                if hi == NB:
                    last.then_inc(out_summed, 1)

            multiply_w(UNITS - 2, 2)
            hidden(NB - 2)
            pe.wait_ge(hid_lo_ready, 1)
            aggregate(0, 0, 0, EARLY)
            transpose_u(UNITS - 1, 3)
            pe.wait_ge(hid_lo_ready, 2)
            aggregate(0, 0, EARLY, BACK)
            multiply_w(UNITS - 1, 3)
            aggregate(1, 1, 0, HALF)
            transpose_h1(NB - 1)
            aggregate(1, 1, HALF, BACK)
            hidden(NB - 1)
            pe.wait_ge(hid_lo_ready, 4)
            aggregate(0, 0, BACK, NB)
            aggregate(1, 1, BACK, NB)
            with pe.Fori(1, NB // 2) as pair:
                for j in range(2):
                    aggregate(2 * pair + j, j)

        @block.vector
        def _(vec):
            chain = [0]

            def link(ins):
                chain[0] += 1
                ins.then_inc(vec_step, 1)
                vec.wait_ge(vec_step, chain[0])

            for g in range(4):
                c = slice(4 * g, 4 * g + 4)
                vec.wait_ge(x_in[g], 16)
                for b in range(4 * g, 4 * g + 4):
                    last = nc.vector.bn_stats(ST[:, b, :], XA[:, b, :])
                link(last)
                for b in range(4 * g, 4 * g + 4):
                    last = nc.vector.bn_aggr(MV[:, b, :], ST[:, b, :])
                link(last)
                nc.vector.tensor_scalar(VE[:, c], MV[:, c, 1], EPS, None, ALU.add).then_inc(x_var_ready, 1)
            for g in range(4):
                c = slice(4 * g, 4 * g + 4)
                vec.wait_ge(x_rstd_ready, g + 1)
                nc.vector.scalar_tensor_tensor(MB[:, c], MV[:, c, 0], -1.0, RS[:, c], ALU.mult, ALU.mult)\
                    .then_inc(x_bias_ready, 1)
            vec.wait_ge(w0_in, 16)
            vec.wait_ge(a0_in, 16)
            for k in range(FK):
                for s in range(2):
                    for h in range(HEADS):
                        link(nc.vector.tensor_tensor_reduce(
                            out=JUNK[:, :], in0=WR[:, k, h, :], in1=AB[:, h, s * F:(s + 1) * F], scale=1.0,
                            scalar=0.0, op0=ALU.mult, op1=ALU.add, accum_out=WA[:, k, s, h:h + 1]))
            vec.sem_inc(wa_ready, 1)
            for g in range(4):
                vec.wait_ge(h_hi_ready, g + 1)
                nc.vector.scalar_tensor_tensor(H[:, 4 * g:4 * g + 4, F:2 * F], XA[:, 4 * g:4 * g + 4, :], H_SCALE,
                                               H[:, 4 * g:4 * g + 4, 0:F], ALU.mult, ALU.subtract)\
                    .then_inc(h_lo_ready, 1)
            for k in range(FK):
                link(nc.vector.tensor_scalar(W[:, k, :, 0:F], WR[:, k, :, :], W_SCALE, None, ALU.mult))
                last = nc.vector.scalar_tensor_tensor(W[:, k, :, F:2 * F], WR[:, k, :, :], W_SCALE,
                                                      W[:, k, :, 0:F], ALU.mult, ALU.subtract)
            last.then_inc(w_lo_ready, 1)
            vec.wait_ge(b1_in, 16)

            def mask_rows(ib):
                vec.wait_ge(adj_in, 16 * (ib + 1))
                if not isinstance(ib, int) or ib >= 1:
                    vec.wait_ge(mask_in, 16 * ib)
                nc.vector.tensor_scalar(MR[:, :], ADJ[:, :], 0.0, None, ALU.not_equal).then_inc(mask_rows_ready, 1)

            mask_rows(0)
            vec.wait_ge(w_lo_ready, 1)
            vec.wait_ge(dst_in[0], 16)
            nc.vector.tensor_tensor(B[:, 0, :], ADJ[:, :], D[:, 0, :], ALU.add).then_inc(adj_dst0_ready, 1)

            def logits(u, h):
                vec.wait_ge(relu_ready, u + 1)
                if isinstance(u, int) and u == 0:
                    vec.wait_ge(adj_dst0_ready, 1)
                else:
                    vec.wait_ge(adj_dst_ready, u)
                if not isinstance(u, int) or u >= HEADS:
                    vec.wait_ge(probs_ready, u - HEADS + 1)
                if not isinstance(u, int):
                    vec.sem_inc(passed_vec, 1)
                nc.vector.tensor_tensor_reduce(out=E[:, h, :], in0=E[:, h, :], in1=B[:, h % 2, :],
                                               scale=-1.0, scalar=3.0e38, op0=ALU.add, op1=ALU.min,
                                               accum_out=nmax[:, h:h + 1]).then_inc(logits_ready, 1)

            def low(v, k, h):
                vec.wait_ge(probs_hi_ready, v + 1)
                if not isinstance(v, int) or v >= 2:
                    vec.wait_ge(lo_in[h % 2], 16 * k)
                nc.vector.scalar_tensor_tensor(PB[:, h % 2, :], E[:, h, :], P_SCALE, PA[:, h % 2, :],
                                               ALU.mult, ALU.subtract).then_inc(probs_lo_ready, 1)

            def row_inverse(u, h):
                vec.wait_ge(probs_ready, u + 1)
                if not isinstance(u, int) or u >= HEADS:
                    vec.wait_ge(u_ready, u - HEADS + 1)
                nc.vector.reciprocal(rinv[:, h:h + 1], rsum[:, h:h + 1]).then_inc(rinv_ready, 1)

            def u_sum(v, h):
                if not isinstance(v, int) or v >= 1:
                    vec.wait_ge(u_transposed, v)
                vec.wait_ge(half_ready, v + 1)
                nc.vector.scalar_tensor_tensor(U[:, :], ACC[h % 2][:, 0:F], rinv[:, h:h + 1], UH[:, :],
                                               ALU.mult, ALU.add).then_inc(u_ready, 1)

            def ut_low(v, h):
                vec.wait_ge(ut_hi_ready, v + 1)
                nc.vector.tensor_tensor(UT[:, 1, :], PU[h % 2], UT[:, 0, :], ALU.subtract).then_inc(ut_lo_ready, 1)

            def mask(ib):
                vec.wait_ge(mask_in, 16 * (ib + 1))
                nc.vector.tensor_scalar(AT[:, :, bass.ds(ib * P, P)], MT[:, :, :], 1.0, None,
                                        ALU.mult).then_inc(mask_ready, 1)

            def x1_block(b):
                vec.wait_ge(xres_in, 16 * (b + 1))
                vec.wait_ge(w_multiplied, 4 * b + 4)
                if not isinstance(b, int) or b >= 1:
                    vec.wait_ge(x1_stored, 16 * b)
                nc.vector.tensor_tensor(XS[:, :], PO[:, F:2 * F], XR[:, :], ALU.add).then_inc(x_sum_ready, 1)
                vec.wait_ge(x_sum_ready, b + 1)
                nc.vector.tensor_tensor(X1[:, :], PO[:, 0:F], XS[:, :], ALU.add).then_inc(x1_ready, 1)
                vec.wait_ge(x1_ready, b + 1)
                nc.vector.bn_stats(stat[:, :], X1[:, :]).then_inc(stat_ready, 1)
                vec.wait_ge(stat_ready, b + 1)
                if not isinstance(b, int):
                    vec.sem_inc(passed_vec, 1)
                nc.vector.bn_aggr(mv[:, :], stat[:, :]).then_inc(mv_ready, 1)
                vec.wait_ge(mv_ready, b + 1)
                nc.vector.tensor_scalar(veps[:, :], mv[:, 1:2], EPS, None, ALU.add).then_inc(veps_ready, 1)

            def norm1(b):
                vec.wait_ge(rstd_ready, b + 1)
                if not isinstance(b, int) or b >= 1:
                    vec.wait_ge(h1_transposed, b)
                nc.vector.tensor_scalar(HN1[:, :], X1[:, :], mv[:, 0:1], rstd[:, 0:1], ALU.subtract, ALU.mult)\
                    .then_inc(norm1_ready, 1)

            def hidden(b):
                if isinstance(b, int) and b == NB - 1:
                    vec.wait_ge(hid_lo_ready, 3)
                elif not isinstance(b, int) or b >= 1:
                    vec.wait_ge(hid_stored, 16 * b)
                vec.wait_ge(hid_summed, b + 1)
                nc.vector.tensor_tensor(HID[:, :], PG, B1[:, :], ALU.add).then_inc(hid_ready, 1)

            def slot(ib, h):
                u = 4 * ib + h
                if has(u + 3):
                    logits(u + 3, (h + 3) % 4)
                if has(u - 2):
                    ut_low(u - 2, (h - 2) % 4)
                if has(u - 1):
                    u_sum(u - 1, (h - 1) % 4)
                if h == 2 and (not isinstance(ib, int) or ib >= 2):
                    hidden(ib - 2)
                if has(u + 2):
                    low(u + 2, 2 * ib + (h + 2) // 2, (h + 2) % 4)
                    row_inverse(u + 2, (h + 2) % 4)
                if h == 1 and not final(ib):
                    mask_rows(ib + 1)
                if h == 1 and (not isinstance(ib, int) or ib >= 1):
                    x1_block(ib - 1)
                if h == 3 and (not isinstance(ib, int) or ib >= 1):
                    norm1(ib - 1)
                if h == 3 and not final(ib):
                    mask(ib + 1)
                if final(ib) and h == 3:
                    hidden_low(1, 0, EARLY, HIN[:, 0:EARLY, :])

            def hidden_low(n, lo, hi, rows):
                vec.wait_ge(hid_hi_ready, n)
                nc.vector.tensor_tensor(HS[:, lo:hi, F:2 * F], rows, HS[:, lo:hi, 0:F],
                                        ALU.subtract).then_inc(hid_lo_ready, 1)

            logits(0, 0)
            logits(1, 1)
            low(0, 0, 0)
            row_inverse(0, 0)
            logits(2, 2)
            low(1, 0, 1)
            row_inverse(1, 1)
            mask(0)

            def body(ib):
                for h in range(HEADS):
                    slot(ib, h)
            block_loop(vec, body)
            def degree(ib):
                nc.vector.tensor_reduce(deg[:, bass.ds(ib, 1)], AT[:, bass.ds(ib, 1), :], mybir.AxisListType.XY,
                                        ALU.add).then_inc(deg_ready, 1)
                vec.wait_ge(deg_ready, ib + 1)
                if not isinstance(ib, int):
                    vec.sem_inc(passed_vec, 1)
                nc.vector.reciprocal(rdeg[:, bass.ds(ib, 1)], deg[:, bass.ds(ib, 1)]).then_inc(rdeg_ready, 1)

            ut_low(UNITS - 2, 2)
            hidden(NB - 2)
            u_sum(UNITS - 1, 3)
            hidden_low(2, EARLY, BACK, HIN[:, EARLY:BACK, :])
            hidden_low(3, NB - 2, NB - 1, HID[:, :].rearrange("p (b f) -> p b f", b=1))
            ut_low(UNITS - 1, 3)
            x1_block(NB - 1)
            norm1(NB - 1)
            degree(0)
            hidden(NB - 1)
            hidden_low(4, NB - 1, NB, HID[:, :].rearrange("p (b f) -> p b f", b=1))
            vec.wait_ge(x1_in, 16)

            def finish(ib, j):
                if not isinstance(ib, int) or ib >= 2:
                    vec.wait_ge(out_stored[j], 8 * (ib - j))
                vec.wait_ge(out_half_ready, ib + 1)
                if not isinstance(ib, int):
                    vec.sem_inc(passed_vec, 1)
                nc.vector.scalar_tensor_tensor(OS[:, j, :], ACC[j][:, 0:F], rdeg[:, bass.ds(ib, 1)], OH[:, j, :],
                                               ALU.mult, ALU.add).then_inc(out_sum_ready, 1)
                vec.wait_ge(out_sum_ready, ib + 1)
                if not isinstance(ib, int):
                    vec.sem_inc(passed_vec, 1)
                res = X1[:, :] if final(ib) else X1R[:, bass.ds(ib, 1), :].rearrange("p b f -> p (b f)")
                nc.vector.tensor_tensor(OUT[:, j, :], OS[:, j, :], res, ALU.add).then_inc(out_ready, 1)

            degree(1)
            finish(0, 0)
            degree(2)
            finish(1, 1)
            with vec.Fori(1, NB // 2 - 1) as pair:
                for j in range(2):
                    degree(2 * pair + j + 1)
                    finish(2 * pair + j, j)
            degree(NB - 1)
            finish(NB - 2, 0)
            finish(NB - 1, 1)


_INS = ["x", "adj", "L0_gnn_W", "L0_gnn_a", "L1_gnn_W", "L1_gnn_b"]


def kernel(**inputs):
    import numpy as np
    import concourse.bacc as bacc
    from concourse.bass_utils import run_bass_kernel_spmd

    nc = bacc.Bacc("TRN2", target_bir_lowering=False, num_devices=1)
    arrays, args = {}, []
    for name in _INS:
        a = np.ascontiguousarray(inputs[name])
        arrays["in_" + name] = a
        args.append(nc.dram_tensor("in_" + name, a.shape, mybir.dt.from_np(a.dtype), kind="ExternalInput").ap())
    out = nc.dram_tensor("out_0", (N, F), mybir.dt.float32, kind="ExternalOutput").ap()
    gnn_kernel(nc, *args, out)
    return run_bass_kernel_spmd(nc, [arrays], core_ids=[0]).results[0]["out_0"]
```

```python
from contextlib import ExitStack

import concourse.bass as bass
from concourse import mybir

P = 128
N = 2048
F = 256
HEADS = 4
NB = N // P
FK = F // P
UNITS = NB * HEADS
BUFS = 4
SLOPE = 0.01
EPS = 1e-5
P_SCALE = 2.0 ** 15
H_SCALE = 2.0 ** 11
W_SCALE = 1.0 / (HEADS * P_SCALE * H_SCALE)


def gnn_kernel(nc, x, adj, w0, a0, w1, b1, out):
    fp32 = mybir.dt.float32
    f32r = mybir.dt.float32r
    fp16 = mybir.dt.float16
    bf16 = mybir.dt.bfloat16
    u8 = mybir.dt.uint8
    ALU = mybir.AluOpType
    ACT = mybir.ActivationFunctionType

    x1_dram = nc.dram_tensor("x1_scratch", (N, F), fp32, kind="Internal").ap()
    hid_dram = nc.dram_tensor("hidden_scratch", (N, F), fp32, kind="Internal").ap()
    dst_dram = nc.dram_tensor("dst_scratch", (HEADS, N), fp32, kind="Internal").ap()

    def blocks(t):
        return t.rearrange("(b p) f -> p b f", p=P)

    ctx = ExitStack()
    with ctx:
        where = {"": (nc.sbuf_base + 63) // 64 * 64}

        def size(shape, dt):
            n = 1
            for s in shape[1:]:
                n *= s
            return n * {fp32: 4, f32r: 4, fp16: 2, bf16: 2, u8: 1}[dt]

        def place(name, shape, dt):
            at = where[""]
            where[name] = at
            where[""] = at + (size(shape, dt) + 31) // 32 * 32
            assert where[""] <= nc.sbuf_usable_end, name
            return nc.alloc_sbuf_tensor_at(name, shape, dt, offset=at)

        def alias(name, shape, dt, over, skip=0):
            return nc.alloc_sbuf_tensor_at(name, shape, dt, offset=where[over] + skip)

        D = place("dst_rows", [P, HEADS, N], fp32)
        AT = place("mask_t", [P, NB, N], u8)
        H = place("h_split", [P, NB, 2 * F], fp16)
        W = place("w0_split", [P, FK, HEADS, 2 * F], f32r)
        E = place("logits", [P, HEADS, N], fp32)
        B = place("adj_dst", [P, 2, N], fp32)
        ADJ = place("adj_rows", [P, N], fp32)
        MR = place("mask_rows", [P, N], bf16)
        MT = place("mask_cols", [P, NB, P], bf16)
        PA = place("probs_hi", [P, 2, N], fp16)
        PB = place("probs_lo", [P, 2, N], fp16)
        TA = place("probs_hi_t", [P, 2, NB, P], fp16)
        TB = place("probs_lo_t", [P, 2, NB, P], fp16)
        U = place("u_rows", [P, F], fp32)
        UH = place("u_half", [P, F], fp32)
        UT = place("u_t", [P, 2, F], f32r)
        W1 = place("w1", [P, FK, F], fp32)
        B1 = place("b1_rows", [P, F], fp32)
        XR = place("x_res", [P, F], fp32)
        X1 = place("x1", [P, F], fp32)
        HN1 = place("x1_norm", [P, F], fp32)
        HT1 = place("h1_t", [P, FK, P], fp32)
        HID = place("hidden", [P, F], fp32)
        ident = place("ident", [P, P], fp32)
        src = place("src_bias", [P, UNITS], fp32)
        nmax = place("neg_max", [P, HEADS], fp32)
        rsum = place("row_sum", [P, HEADS], fp32)
        power = place("power", [P, 4], fp32)
        veps = place("var_eps", [P, 1], fp32)
        rinv = place("row_inv", [P, HEADS], fp32)
        stat = place("stat", [P, 6], fp32)
        mv = place("mean_var", [P, 2], fp32)
        rstd = place("rstd", [P, 1], fp32)
        deg = place("deg", [P, NB], fp32)
        rdeg = place("rdeg", [P, NB], fp32)

        XA = alias("x_all", [P, NB, F], fp32, "logits", 4 * 2 * N)
        WR = alias("w0_raw", [P, FK, HEADS, F], fp32, "adj_dst")
        AB = alias("a_rows", [P, HEADS, 2 * F], fp32, "adj_dst", 4 * N)
        HT = alias("h_t", [P, FK, N], fp32, "probs_hi_t")
        o = 0
        WA = alias("wa", [P, FK, 2, HEADS], fp32, "probs_lo", o)
        o += 4 * FK * 2 * HEADS
        ST = alias("x_stats", [P, NB, 6], fp32, "probs_lo", o)
        o += 4 * NB * 6
        MV = alias("x_mean_var", [P, NB, 2], fp32, "probs_lo", o)
        o += 4 * NB * 2
        VE = alias("x_var_eps", [P, NB], fp32, "probs_lo", o)
        o += 4 * NB
        RS = alias("x_rstd", [P, NB], fp32, "probs_lo", o)
        o += 4 * NB
        MB = alias("x_bias", [P, NB], fp32, "probs_lo", o)
        o += 4 * NB
        JUNK = alias("junk", [P, FK * 2 * HEADS, F], fp32, "logits")
        SD = alias("src_dst_rows", [2 * HEADS, N], fp32, "probs_hi")
        HIN = alias("hidden_in", [P, NB, F], fp32, "adj_dst")
        HS = alias("hidden_split", [P, NB, 2 * F], f32r, "logits")
        X1R = alias("x1_in", [P, NB, F], fp32, "h_split")
        MC = alias("mask_columns", [P, BUFS, NB, P], f32r, "probs_hi")
        OH = alias("out_half", [P, BUFS, F], fp32, "dst_rows")
        OX = alias("out_half_x1", [P, BUFS, F], fp32, "dst_rows", 4 * BUFS * F)
        OUT = alias("out_rows", [P, 2, F], fp32, "dst_rows", 8 * BUFS * F)

        def psum(name, cols):
            return ctx.enter_context(nc.psum_tensor(name, [P, cols], fp32))

        PP = [psum(f"ps_pair{i}", 4 * F) for i in range(2)]
        PU = [t[:, 0:F] for t in PP]
        PH, PG = PP[0][:, 2 * F:3 * F], PP[1][:, 2 * F:3 * F]
        ACC = [psum(f"ps_acc{i}", 2 * F) for i in range(2)]
        PO = psum("ps_out", 2 * F)
        PX = psum("ps_rows", 2 * F)
        PD = [PP[1][:, 0:4 * P], PP[1][:, 4 * P:8 * P], ACC[0], ACC[1]]
        PS = [ACC[0], ACC[1], PO, PX]

        def sem(name):
            return ctx.enter_context(nc.semaphore(name))

        x_in = [sem(f"x_in{g}") for g in range(4)]
        w0_in, a0_in, w1_in, b1_in = sem("w0_in"), sem("a0_in"), sem("w1_in"), sem("b1_in")
        adj_in, xres_in = sem("adj_in"), sem("xres_in")
        x1_stored, hid_stored = sem("x1_stored"), sem("hid_stored")
        hid_in = [sem(f"hid_in{n}") for n in range(3)]
        x1_in, out_stored = sem("x1_in"), [sem("out_stored0"), sem("out_stored1")]
        dst_stored, dst_in = sem("dst_stored"), [None] + [sem(f"dst_in{h}") for h in range(1, HEADS)]
        zeroed, ident_ready, power_ready = sem("zeroed"), sem("ident_ready"), sem("power_ready")
        vec_step = sem("vec_step")
        x_veps_ready = sem("x_veps_ready")
        x_var_ready, x_rstd_ready, x_bias_ready = sem("x_var_ready"), sem("x_rstd_ready"), sem("x_bias_ready")
        h_ready, h_hi_ready, h_lo_ready = sem("h_ready"), sem("h_hi_ready"), sem("h_lo_ready")
        h_transposed, ht_ready = sem("h_transposed"), sem("ht_ready")
        wa_ready, w_lo_ready = sem("wa_ready"), sem("w_lo_ready")
        sd_summed, sd_ready = sem("sd_summed"), sem("sd_ready")
        dst0_spread, dst0_ready = sem("dst0_spread"), sem("dst0_ready")
        src_transposed, src_ready = sem("src_transposed"), sem("src_ready")
        adj_dst0_ready = sem("adj_dst0_ready")
        adj_dst_ready = sem("adj_dst_ready")
        relu_ready = sem("relu_ready")
        logits_ready = sem("logits_ready")
        probs_ready = sem("probs_ready")
        rinv_ready = sem("rinv_ready")
        probs_hi_ready, probs_lo_ready = sem("probs_hi_ready"), sem("probs_lo_ready")
        hi_in = [sem("hi_in0"), sem("hi_in1")]
        lo_in = [sem("lo_in0"), sem("lo_in1")]
        hi_multiplied, unit_multiplied = sem("hi_multiplied"), sem("unit_multiplied")
        half_ready, u_ready = sem("half_ready"), sem("u_ready")
        u_transposed, ut_hi_ready, ut_lo_ready = sem("u_transposed"), sem("ut_hi_ready"), sem("ut_lo_ready")
        w_multiplied = sem("w_multiplied")
        mask_rows_ready = sem("mask_rows_ready")
        mask_in, mask_ready = sem("mask_in"), sem("mask_ready")
        x1_ready, stat_ready, mv_ready = sem("x1_ready"), sem("stat_ready"), sem("mv_ready")
        veps_ready, rstd_ready = sem("veps_ready"), sem("rstd_ready")
        norm1_ready, h1_transposed, h1_ready, hid_summed, hid_ready = (
            sem("norm1_ready"), sem("h1_transposed"), sem("h1_ready"), sem("hid_summed"),
            sem("hid_ready"))
        hid_hi_ready, hid_lo_ready = sem("hid_hi_ready"), sem("hid_lo_ready")
        cast_ready, out_summed = sem("cast_ready"), sem("out_summed")
        out_half_ready, half_x1_ready = sem("out_half_ready"), sem("half_x1_ready")
        deg_ready, rdeg_ready, out_ready = sem("deg_ready"), sem("rdeg_ready"), sem("out_ready")
        passed_vec, passed_act, passed_pool, passed_sp = (
            sem("passed_vec"), sem("passed_act"), sem("passed_pool"), sem("passed_sp"))

        HALF = NB // 2
        BACK = NB - 2
        EARLY = BACK - 1
        PARTS = [(0, HALF), (HALF, EARLY), (EARLY, BACK)]
        AC = [ACC[0], ACC[1], PX, PO]

        def has(u):
            return not isinstance(u, int) or 0 <= u < UNITS

        def block_loop(eng, body, first=3, last=2):
            for ib in range(first):
                body(ib)
            with eng.Fori(first, NB - last) as ib:
                body(ib)
            for ib in range(NB - last, NB):
                body(ib)

        def final(ib):
            return isinstance(ib, int) and ib == NB - 1

        block = ctx.enter_context(nc.Block())

        @block.sync
        def _(sp):
            for g in range(4):
                sp.dma_start(XA[:, 4 * g:4 * g + 4, :], blocks(x)[:, 4 * g:4 * g + 4, :]).then_inc(x_in[g], 16)
            sp.dma_start(AB[:, :, :].rearrange("p h d -> p (h d)"),
                         a0.rearrange("h d o -> (h d o)").partition_broadcast(P)).then_inc(a0_in, 16)
            sp.dma_start(WR[:, :, :, :], w0.rearrange("(k p) (h d) -> p k h d", p=P, h=HEADS)).then_inc(w0_in, 16)
            sp.dma_start(ADJ[:, :], adj[0:P, :]).then_inc(adj_in, 16)
            sp.dma_start(W1[:, :, :], w1.rearrange("(k p) f -> p k f", p=P)).then_inc(w1_in, 16)
            sp.dma_start(B1[:, :], b1.partition_broadcast(P)).then_inc(b1_in, 16)

            def passed(b):
                if not isinstance(b, int):
                    sp.sem_inc(passed_sp, 1)

            def store_hidden(b):
                sp.wait_ge(hid_ready, b + 1)
                passed(b)
                sp.dma_start(hid_dram[bass.ds(b * P, P), :], HID[:, :]).then_inc(hid_stored, 16)

            def store_x1(b):
                sp.wait_ge(x1_ready, b + 1)
                passed(b)
                sp.dma_start(x1_dram[bass.ds(b * P, P), :], X1[:, :]).then_inc(x1_stored, 16)

            def load_adj(ib):
                sp.wait_ge(adj_dst_ready, 4 * ib - 2)
                passed(ib)
                sp.wait_ge(mask_rows_ready, ib)
                passed(ib)
                sp.dma_start(ADJ[:, :], adj[bass.ds(ib * P, P), :]).then_inc(adj_in, 16)

            def transpose_hi(u, e):
                sp.wait_ge(probs_hi_ready, u + 1)
                passed(u)
                if not isinstance(u, int) or u >= 2:
                    sp.wait_ge(hi_multiplied, u - 1)
                    passed(u)
                sp.dma_start_transpose(TA[:, e, :, :], PA[:, e, :]).then_inc(hi_in[e], 16)

            def transpose_lo(u, e):
                sp.wait_ge(probs_lo_ready, u + 1)
                passed(u)
                if not isinstance(u, int) or u >= 2:
                    sp.wait_ge(unit_multiplied, u - 1)
                    passed(u)
                sp.dma_start_transpose(TB[:, e, :, :], PB[:, e, :]).then_inc(lo_in[e], 16)

            def transpose_mask(b):
                sp.wait_ge(mask_rows_ready, b + 1)
                passed(b)
                if not isinstance(b, int) or b >= 1:
                    sp.wait_ge(mask_ready, b)
                    passed(b)
                sp.dma_start_transpose(MT[:, :, :], MR[:, :]).then_inc(mask_in, 16)

            def load_hidden(lo, hi, n):
                sp.dma_start(HIN[:, lo:hi, :], blocks(hid_dram)[:, lo:hi, :]).then_inc(hid_in[n], 16)

            def slot(ib, h):
                u = 4 * ib + h
                if has(u + 2):
                    transpose_hi(u + 2, h % 2)
                if h == 2 and isinstance(ib, int) and ib == 0:
                    load_adj(2)
                if h == 3:
                    if not isinstance(ib, int) or ib >= 2:
                        store_hidden(ib - 2)
                    if not isinstance(ib, int) or ib >= 1:
                        store_x1(ib - 1)
                    sp.dma_start(XR[:, :], x[bass.ds(ib * P, P), :]).then_inc(xres_in, 16)
                if has(u + 2):
                    transpose_lo(u + 2, h % 2)
                if h == 1 and not (isinstance(ib, int) and (ib == 0 or ib + 2 >= NB)):
                    load_adj(ib + 2)
                if h == 1 and not final(ib):
                    transpose_mask(ib + 1)
                if final(ib) and h <= 1:
                    if h == 0:
                        sp.wait_ge(hid_stored, 16 * EARLY)
                        sp.wait_ge(logits_ready, UNITS)
                    load_hidden(*PARTS[h], h)

            transpose_mask(0)
            sp.wait_ge(sd_ready, 4)
            sp.dma_start(dst_dram, SD[HEADS:2 * HEADS, :]).then_inc(dst_stored, 16)
            sp.wait_ge(dst_stored, 16)
            for h in range(1, HEADS):
                sp.dma_start(D[:, h, :], dst_dram[h, :].partition_broadcast(P)).then_inc(dst_in[h], 16)
            transpose_hi(0, 0)
            transpose_lo(0, 0)
            load_adj(1)
            transpose_hi(1, 1)
            transpose_lo(1, 1)

            def body(ib):
                for h in range(HEADS):
                    slot(ib, h)
            block_loop(sp, body)
            sp.wait_ge(hid_stored, 16 * BACK)
            load_hidden(*PARTS[2], 2)
            sp.wait_ge(x1_stored, 16 * (NB - 1))
            sp.wait_ge(unit_multiplied, UNITS)
            sp.dma_start(X1R[:, 0:NB - 1, :], blocks(x1_dram)[:, 0:NB - 1, :]).then_inc(x1_in, 16)

            def store(ib, j):
                sp.wait_ge(out_ready, ib + 1)
                passed(ib)
                sp.dma_start(out[bass.ds(ib * P, P), :], OUT[:, j, :]).then_inc(out_stored[j], 16)
            with sp.Fori(0, NB // 2) as pair:
                for j in range(2):
                    store(2 * pair + j, j)
            for j in range(2):
                sp.wait_ge(out_stored[j], 8 * NB)

        @block.gpsimd
        def _(pool):
            nc.gpsimd.memset(ident[:, :], 0.0).then_inc(zeroed, 1)
            nc.gpsimd.memset(power[:, :], -0.5).then_inc(power_ready, 1)
            pool.wait_ge(zeroed, 1)
            nc.gpsimd.affine_select(out=ident[:, :], in_=ident[:, :], compare_op=ALU.not_equal, fill=1.0,
                                    base=0, pattern=[[-1, P]], channel_multiplier=1).then_inc(ident_ready, 1)
            pool.wait_ge(power_ready, 1)
            for g in range(4):
                c = slice(4 * g, 4 * g + 4)
                pool.wait_ge(x_var_ready, g + 1)
                nc.gpsimd.tensor_scalar(VE[:, c], MV[:, c, 1], EPS, None, ALU.add).then_inc(x_veps_ready, 1)
                pool.wait_ge(x_veps_ready, g + 1)
                nc.gpsimd.tensor_tensor(RS[:, c], VE[:, c], power[:, :], ALU.pow).then_inc(x_rstd_ready, 1)

            for g in range(4):
                pool.wait_ge(h_ready, g + 1)
                nc.gpsimd.tensor_scalar(H[:, 4 * g:4 * g + 4, 0:F], XA[:, 4 * g:4 * g + 4, :], H_SCALE, None,
                                        ALU.mult).then_inc(h_hi_ready, 1)

            def adj_dst(ib, h):
                u = 4 * ib + h
                if h == 0:
                    pool.wait_ge(adj_in, 16 * (ib + 1))
                if isinstance(u, int) and u < HEADS:
                    pool.wait_ge(dst_in[h], 16)
                pool.wait_ge(logits_ready, u - 1)
                pool.sem_inc(passed_pool, 1)
                nc.gpsimd.tensor_tensor(B[:, h % 2, :], ADJ[:, :], D[:, h, :], ALU.add).then_inc(adj_dst_ready, 1)

            def rstd_of(b):
                pool.wait_ge(mv_ready, b + 1)
                pool.sem_inc(passed_pool, 1)
                nc.gpsimd.tensor_scalar(veps[:, :], mv[:, 1:2], EPS, None, ALU.add).then_inc(veps_ready, 1)
                pool.wait_ge(veps_ready, b + 1)
                pool.sem_inc(passed_pool, 1)
                nc.gpsimd.tensor_tensor(rstd[:, :], veps[:, :], power[:, 0:1], ALU.pow).then_inc(rstd_ready, 1)

            def body(ib):
                for h in range(HEADS):
                    if not isinstance(ib, int) or ib >= 1 or h >= 2:
                        adj_dst(ib, h)
                if not isinstance(ib, int) or ib >= 2:
                    rstd_of(ib - 2)
            block_loop(pool, body)
            rstd_of(NB - 2)
            rstd_of(NB - 1)

            def half_x1(ib, j):
                pool.wait_ge(out_half_ready, ib + 1)
                pool.sem_inc(passed_pool, 1)
                if not isinstance(ib, int) or ib >= BUFS:
                    pool.wait_ge(out_ready, ib - BUFS + 1)
                    pool.sem_inc(passed_pool, 1)
                res = X1[:, :] if final(ib) else X1R[:, bass.ds(ib, 1), :].rearrange("p b f -> p (b f)")
                nc.gpsimd.tensor_tensor(OX[:, j, :], OH[:, j, :], res, ALU.add).then_inc(half_x1_ready, 1)

            pool.wait_ge(x1_in, 16)
            pool.wait_ge(x1_ready, NB)
            for j in range(BUFS):
                half_x1(j, j)
            with pool.Fori(1, NB // BUFS - 1) as quad:
                for j in range(BUFS):
                    half_x1(BUFS * quad + j, j)
            for j in range(BUFS):
                half_x1(NB - BUFS + j, j)

        @block.scalar
        def _(act):
            def h_relu(g):
                act.wait_ge(x_bias_ready, g + 1)
                for b in range(4 * g, 4 * g + 4):
                    last = nc.scalar.activation(XA[:, b, :], XA[:, b, :], ACT.Relu, scale=RS[:, b:b + 1],
                                                bias=MB[:, b:b + 1])
                last.then_inc(h_ready, 1)

            def h_columns(g):
                act.wait_ge(h_transposed, g + 1)
                nc.scalar.activation(
                    HT[:, :, 4 * g * P:(4 * g + 4) * P].rearrange("p k (b c) -> p b k c", b=4),
                    PP[g % 2][:, :].rearrange("p (b k c) -> p b k c", b=4, k=FK),
                    ACT.Copy).then_inc(ht_ready, 1)

            h_relu(0)
            h_relu(1)
            h_columns(0)
            h_relu(2)
            h_columns(1)
            h_relu(3)
            h_columns(2)
            h_columns(3)

            def dst0_rows(g):
                act.wait_ge(dst0_spread, g + 1)
                nc.scalar.activation(D[:, 0, 4 * g * P:(4 * g + 4) * P], PD[g][:, 0:4 * P], ACT.Copy)\
                    .then_inc(dst0_ready, 1)

            for g in range(4):
                act.wait_ge(sd_summed, g + 1)
                nc.scalar.activation(SD[:, 4 * g * P:(4 * g + 4) * P], PS[g][0:2 * HEADS, :], ACT.Copy)\
                    .then_inc(sd_ready, 1)
                if g >= 1:
                    dst0_rows(g - 1)
            dst0_rows(3)
            act.wait_ge(src_transposed, 1)
            nc.scalar.activation(
                src[:, :].rearrange("p (b h) -> p b h", h=HEADS),
                PP[0][:, 0:NB * 2 * HEADS].rearrange("p (b s h) -> p b s h", s=2, h=HEADS)[:, :, 0, :],
                ACT.Copy, scale=-(1.0 - SLOPE)).then_inc(src_ready, 1)

            def relu_term(u, h):
                if isinstance(u, int) and u < HEADS:
                    if u == 0:
                        act.wait_ge(src_ready, 1)
                        act.wait_ge(dst0_ready, 4)
                    if u == 2:
                        act.wait_ge(h_hi_ready, 4)
                        act.wait_ge(h_lo_ready, 4)
                else:
                    act.wait_ge(probs_lo_ready, u - HEADS + 1)
                if isinstance(u, int) and 1 <= u < HEADS:
                    act.wait_ge(dst_in[u], 16)
                if not isinstance(u, int):
                    act.sem_inc(passed_act, 1)
                nc.scalar.activation(E[:, h, :], D[:, h, :], ACT.Relu, scale=-(1.0 - SLOPE),
                                     bias=src[:, bass.ds(u, 1)]).then_inc(relu_ready, 1)

            def exp(u, h):
                act.wait_ge(logits_ready, u + 1)
                if not isinstance(u, int) or u >= HEADS:
                    act.wait_ge(rinv_ready, u - HEADS + 1)
                nc.scalar.activation(E[:, h, :], E[:, h, :], ACT.Exp, scale=-1.0,
                                     bias=nmax[:, h:h + 1], accum_out=rsum[:, h:h + 1]).then_inc(probs_ready, 1)

            def high(v, k, h):
                act.wait_ge(probs_ready, v + 1)
                if not isinstance(v, int) or v >= 2:
                    act.wait_ge(hi_in[h % 2], 16 * k)
                nc.scalar.activation(PA[:, h % 2, :], E[:, h, :], ACT.Copy, scale=P_SCALE)\
                    .then_inc(probs_hi_ready, 1)

            def u_half(v, h):
                act.wait_ge(rinv_ready, v + 1)
                if not isinstance(v, int) or v >= 1:
                    act.wait_ge(u_ready, v)
                act.wait_ge(unit_multiplied, v + 1)
                nc.scalar.activation(UH[:, :], ACC[h % 2][:, F:2 * F], ACT.Copy,
                                     scale=rinv[:, h:h + 1]).then_inc(half_ready, 1)

            def ut_high(v, h):
                if not isinstance(v, int) or v >= 1:
                    act.wait_ge(w_multiplied, v)
                act.wait_ge(u_transposed, v + 1)
                nc.scalar.activation(UT[:, 0, :], PU[h % 2], ACT.Copy).then_inc(ut_hi_ready, 1)

            def h1_relu(b):
                if not isinstance(b, int) or b >= 1:
                    act.wait_ge(hid_summed, b)
                act.wait_ge(h1_transposed, b + 1)
                nc.scalar.activation(HT1[:, :, :], PH.rearrange("p (k c) -> p k c", k=FK),
                                     ACT.Relu).then_inc(h1_ready, 1)

            def slot(ib, h):
                u = 4 * ib + h
                if has(u - 2):
                    ut_high(u - 2, (h - 2) % 4)
                if has(u - 1):
                    u_half(u - 1, (h - 1) % 4)
                if has(u + 2):
                    high(u + 2, 2 * ib + (h + 2) // 2, (h + 2) % 4)
                if h == 0 and (not isinstance(ib, int) or ib >= 2):
                    h1_relu(ib - 2)
                if has(u + 3):
                    exp(u + 3, (h + 3) % 4)
                if has(u + 5):
                    relu_term(u + 5, (h + 1) % 4)
                if final(ib) and h == 2:
                    cast(0, 0)
                    for n in range(2):
                        act.wait_ge(hid_in[n], 16)
                        hidden_high(*PARTS[n], HIN[:, PARTS[n][0]:PARTS[n][1], :])
                if final(ib) and h == 3:
                    cast(1, 1)

            def cast(ib, j):
                if not isinstance(ib, int) or ib >= BUFS:
                    act.wait_ge(out_summed, ib - BUFS + 1)
                    act.sem_inc(passed_act, 1)
                elif ib < 2:
                    act.wait_ge(mask_ready, NB)
                    act.wait_ge(probs_lo_ready, UNITS)
                    for e in range(2):
                        act.wait_ge((hi_in, lo_in)[ib][e], 16 * UNITS // 2)
                else:
                    act.wait_ge((hi_multiplied, unit_multiplied)[ib - 2], UNITS)
                nc.scalar.activation(MC[:, j, :, :], AT[:, :, bass.ds(ib * P, P)], ACT.Copy).then_inc(cast_ready, 1)

            def hidden_high(lo, hi, rows):
                nc.scalar.activation(HS[:, lo:hi, 0:F], rows, ACT.Copy).then_inc(hid_hi_ready, 1)

            relu_term(0, 0)
            relu_term(1, 1)
            exp(0, 0)
            high(0, 0, 0)
            relu_term(2, 2)
            exp(1, 1)
            high(1, 0, 1)
            relu_term(3, 3)
            exp(2, 2)
            relu_term(4, 0)

            def body(ib):
                for h in range(HEADS):
                    slot(ib, h)
            block_loop(act, body)
            u_half(UNITS - 1, 3)
            ut_high(UNITS - 2, 2)
            h1_relu(NB - 2)
            act.wait_ge(hid_in[2], 16)
            hidden_high(*PARTS[2], HIN[:, EARLY:BACK, :])
            cast(2, 2)
            ut_high(UNITS - 1, 3)
            act.wait_ge(hid_ready, NB - 1)
            hidden_high(NB - 2, NB - 1, HID[:, :].rearrange("p (b f) -> p b f", b=1))
            cast(3, 3)
            h1_relu(NB - 1)
            act.wait_ge(hid_ready, NB)
            hidden_high(NB - 1, NB, HID[:, :].rearrange("p (b f) -> p b f", b=1))

            def out_half(ib, j):
                if not isinstance(ib, int) or ib >= BUFS:
                    act.wait_ge(half_x1_ready, ib - BUFS + 1)
                act.wait_ge(rdeg_ready, ib + 1)
                act.wait_ge(out_summed, ib + 1)
                if not isinstance(ib, int):
                    act.sem_inc(passed_act, 1)
                nc.scalar.activation(OH[:, j, :], AC[j][:, F:2 * F], ACT.Copy,
                                     scale=rdeg[:, bass.ds(ib, 1)]).then_inc(out_half_ready, 1)

            for j in range(BUFS):
                out_half(j, j)
                cast(j + BUFS, j)
            with act.Fori(1, NB // BUFS - 1) as quad:
                for j in range(BUFS):
                    out_half(BUFS * quad + j, j)
                    cast(BUFS * quad + j + BUFS, j)
            for j in range(BUFS):
                out_half(NB - BUFS + j, j)

        @block.tensor
        def _(pe):
            def keep_warm(n, moving, stationary):
                for _ in range(n):
                    nc.tensor.matmul(PX[:, 0:moving.shape[-1]], stationary, moving, start=True, stop=True)

            pe.wait_ge(ident_ready, 1)
            pe.wait_ge(x_in[1], 16)
            keep_warm(16, ident[:, :], ident[:, :])
            for g in range(4):
                pe.wait_ge(h_ready, g + 1)
                if g >= 2:
                    pe.wait_ge(ht_ready, g - 1)
                for b in range(4):
                    for k in range(FK):
                        c = (b * FK + k) * P
                        last = nc.tensor.transpose(PP[g % 2][:, c:c + P], XA[:, 4 * g + b, k * P:(k + 1) * P],
                                                   ident[:, :])
                last.then_inc(h_transposed, 1)
                if g < 3:
                    keep_warm(6, ident[:, :], ident[:, :])

            def spread_dst0(g):
                pe.wait_ge(sd_ready, g + 1)
                pick = ident[0:2 * HEADS, HEADS:HEADS + 1].to_broadcast([2 * HEADS, P])
                nc.tensor.matmul(PD[g][:, 0:4 * P], pick, SD[:, 4 * g * P:(4 * g + 4) * P],
                                 start=True, stop=True).then_inc(dst0_spread, 1)

            pe.wait_ge(wa_ready, 1)
            for g in range(4):
                pe.wait_ge(ht_ready, g + 1)
                for k in range(FK):
                    last = nc.tensor.matmul(PS[g][0:2 * HEADS, :], WA[:, k, :, :], HT[:, k, 4 * g * P:(4 * g + 4) * P],
                                            start=(k == 0), stop=(k == FK - 1))
                last.then_inc(sd_summed, 1)
                if g >= 1:
                    spread_dst0(g - 1)
            spread_dst0(3)
            for b in range(NB):
                last = nc.tensor.transpose(PP[0][:, b * 2 * HEADS:(b + 1) * 2 * HEADS], SD[:, b * P:(b + 1) * P],
                                           ident[0:2 * HEADS, 0:2 * HEADS])
            last.then_inc(src_transposed, 1)

            def multiply(u, k, h):
                e = h % 2
                pe.wait_ge(hi_in[e], 16 * (k + 1))
                if not isinstance(u, int) or u >= 2:
                    pe.wait_ge(u_ready, u - 1)
                for b in range(NB):
                    last = nc.tensor.matmul(ACC[e][:, :], TA[:, e, b, :], H[:, b, :], start=(b == 0), stop=False)
                last.then_inc(hi_multiplied, 1)

            def multiply_low(k, h):
                e = h % 2
                pe.wait_ge(lo_in[e], 16 * (k + 1))
                for b in range(NB):
                    last = nc.tensor.matmul(ACC[e][:, F:2 * F], TB[:, e, b, :], H[:, b, 0:F],
                                            start=False, stop=(b == NB - 1))
                last.then_inc(unit_multiplied, 1)

            def transpose_u(v, h):
                pe.wait_ge(u_ready, v + 1)
                for k in range(FK):
                    last = nc.tensor.transpose(PU[h % 2][:, k * P:(k + 1) * P], U[:, k * P:(k + 1) * P], ident[:, :])
                last.then_inc(u_transposed, 1)

            def multiply_w(v, h):
                pe.wait_ge(ut_hi_ready, v + 1)
                for k in range(FK):
                    for part in range(2):
                        nc.tensor.matmul(PO[:, 0:F], UT[:, 0, k * P:(k + 1) * P],
                                         W[:, k, h, part * F:(part + 1) * F],
                                         start=(h == 0 and k == 0 and part == 0), stop=False)
                pe.wait_ge(ut_lo_ready, v + 1)
                for k in range(FK):
                    last = nc.tensor.matmul(PO[:, 0:F], UT[:, 1, k * P:(k + 1) * P], W[:, k, h, 0:F],
                                            start=False, stop=(h == HEADS - 1 and k == FK - 1))
                last.then_inc(w_multiplied, 1)

            def transpose_h1(b):
                pe.wait_ge(norm1_ready, b + 1)
                if not isinstance(b, int) or b >= 1:
                    pe.wait_ge(h1_ready, b)
                for k in range(FK):
                    last = nc.tensor.transpose(PH[:, k * P:(k + 1) * P], HN1[:, k * P:(k + 1) * P], ident[:, :])
                last.then_inc(h1_transposed, 1)

            def hidden(b):
                pe.wait_ge(h1_ready, b + 1)
                if not isinstance(b, int) or b >= 1:
                    pe.wait_ge(hid_ready, b)
                for k in range(FK):
                    last = nc.tensor.matmul(PG, HT1[:, k, :], W1[:, k, :],
                                            start=(k == 0), stop=(k == FK - 1))
                last.then_inc(hid_summed, 1)

            def slot(ib, h):
                u = 4 * ib + h
                multiply(u, 2 * ib + h // 2, h)
                if has(u - 2):
                    if h == 2 and (not isinstance(ib, int) or ib >= 1):
                        pe.wait_ge(x1_ready, ib)
                    multiply_w(u - 2, (h - 2) % 4)
                if h == 1 and (not isinstance(ib, int) or ib >= 2):
                    hidden(ib - 2)
                multiply_low(2 * ib + h // 2, h)
                if h == 3 and (not isinstance(ib, int) or ib >= 1):
                    transpose_h1(ib - 1)
                if has(u - 1):
                    transpose_u(u - 1, (h - 1) % 4)

            pe.wait_ge(w_lo_ready, 1)
            pe.wait_ge(h_lo_ready, 4)
            pe.wait_ge(w1_in, 16)
            pe.wait_ge(probs_hi_ready, 1)
            keep_warm(9, H[:, 0, :], H[:, 0, 0:P])

            def body(ib):
                for h in range(HEADS):
                    slot(ib, h)
            block_loop(pe, body)

            def aggregate(ib, j, lo=0, hi=NB):
                if lo == 0:
                    pe.wait_ge(cast_ready, ib + 1)
                    if not isinstance(ib, int) or ib >= BUFS:
                        pe.wait_ge(out_ready, ib - BUFS + 1)
                for b in range(lo, hi):
                    last = nc.tensor.matmul(AC[j][:, :], MC[:, j, b, :], HS[:, b, :],
                                            start=(b == 0), stop=(b == NB - 1))
                if hi == NB:
                    last.then_inc(out_summed, 1)

            pe.wait_ge(hid_lo_ready, 1)
            aggregate(0, 0, 0, HALF)
            multiply_w(UNITS - 2, 2)
            transpose_u(UNITS - 1, 3)
            hidden(NB - 2)
            pe.wait_ge(hid_lo_ready, 2)
            aggregate(0, 0, HALF, EARLY)
            multiply_w(UNITS - 1, 3)
            aggregate(1, 1, 0, EARLY)
            transpose_h1(NB - 1)
            aggregate(2, 2, 0, EARLY)
            hidden(NB - 1)
            pe.wait_ge(hid_lo_ready, 4)
            for j in range(3):
                aggregate(j, j, EARLY, NB - 1)
            pe.wait_ge(hid_lo_ready, 5)
            for j in range(3):
                aggregate(j, j, NB - 1, NB)
            aggregate(3, 3)
            with pe.Fori(1, NB // BUFS) as quad:
                for j in range(BUFS):
                    aggregate(BUFS * quad + j, j)

        @block.vector
        def _(vec):
            chain = [0]

            def link(ins):
                chain[0] += 1
                ins.then_inc(vec_step, 1)
                vec.wait_ge(vec_step, chain[0])

            def x_bias(g):
                c = slice(4 * g, 4 * g + 4)
                vec.wait_ge(x_rstd_ready, g + 1)
                nc.vector.scalar_tensor_tensor(MB[:, c], MV[:, c, 0], -1.0, RS[:, c], ALU.mult, ALU.mult)\
                    .then_inc(x_bias_ready, 1)

            def mask_rows(ib):
                vec.wait_ge(adj_in, 16 * (ib + 1))
                if not isinstance(ib, int) or ib >= 1:
                    vec.wait_ge(mask_in, 16 * ib)
                nc.vector.tensor_scalar(MR[:, :], ADJ[:, :], 0.0, None, ALU.not_equal).then_inc(mask_rows_ready, 1)

            for g in range(4):
                vec.wait_ge(x_in[g], 16)
                for b in range(4 * g, 4 * g + 4):
                    last = nc.vector.bn_stats(ST[:, b, :], XA[:, b, :])
                link(last)
                for b in range(4 * g, 4 * g + 4):
                    last = nc.vector.bn_aggr(MV[:, b, :], ST[:, b, :])
                last.then_inc(x_var_ready, 1)
                if g >= 1:
                    x_bias(g - 1)
            x_bias(3)
            vec.wait_ge(w0_in, 16)
            vec.wait_ge(a0_in, 16)
            for k in range(FK):
                for s in range(2):
                    for h in range(HEADS):
                        last = nc.vector.tensor_tensor_reduce(
                            out=JUNK[:, (k * 2 + s) * HEADS + h, :], in0=WR[:, k, h, :],
                            in1=AB[:, h, s * F:(s + 1) * F], scale=1.0,
                            scalar=0.0, op0=ALU.mult, op1=ALU.add, accum_out=WA[:, k, s, h:h + 1])
            last.then_inc(wa_ready, 1)
            mask_rows(0)
            for k in range(FK):
                link(nc.vector.tensor_scalar(W[:, k, :, 0:F], WR[:, k, :, :], W_SCALE, None, ALU.mult))
                last = nc.vector.scalar_tensor_tensor(W[:, k, :, F:2 * F], WR[:, k, :, :], W_SCALE,
                                                      W[:, k, :, 0:F], ALU.mult, ALU.subtract)
            last.then_inc(w_lo_ready, 1)
            vec.wait_ge(b1_in, 16)

            for g in range(4):
                vec.wait_ge(h_hi_ready, g + 1)
                nc.vector.scalar_tensor_tensor(H[:, 4 * g:4 * g + 4, F:2 * F], XA[:, 4 * g:4 * g + 4, :], H_SCALE,
                                               H[:, 4 * g:4 * g + 4, 0:F], ALU.mult, ALU.subtract)\
                    .then_inc(h_lo_ready, 1)

            def adj_dst(u):
                if u == 0:
                    vec.wait_ge(dst0_ready, 4)
                else:
                    vec.wait_ge(dst_in[u], 16)
                nc.vector.tensor_tensor(B[:, u, :], ADJ[:, :], D[:, u, :], ALU.add).then_inc(adj_dst0_ready, 1)

            def logits(u, h):
                vec.wait_ge(relu_ready, u + 1)
                if isinstance(u, int) and u < 2:
                    vec.wait_ge(adj_dst0_ready, u + 1)
                else:
                    vec.wait_ge(adj_dst_ready, u - 1)
                if not isinstance(u, int) or u >= HEADS:
                    vec.wait_ge(probs_ready, u - HEADS + 1)
                if not isinstance(u, int):
                    vec.sem_inc(passed_vec, 1)
                nc.vector.tensor_tensor_reduce(out=E[:, h, :], in0=E[:, h, :], in1=B[:, h % 2, :],
                                               scale=-1.0, scalar=3.0e38, op0=ALU.add, op1=ALU.min,
                                               accum_out=nmax[:, h:h + 1]).then_inc(logits_ready, 1)

            def low(v, k, h):
                vec.wait_ge(probs_hi_ready, v + 1)
                if not isinstance(v, int) or v >= 2:
                    vec.wait_ge(lo_in[h % 2], 16 * k)
                nc.vector.scalar_tensor_tensor(PB[:, h % 2, :], E[:, h, :], P_SCALE, PA[:, h % 2, :],
                                               ALU.mult, ALU.subtract).then_inc(probs_lo_ready, 1)

            def row_inverse(u, h):
                vec.wait_ge(probs_ready, u + 1)
                if not isinstance(u, int) or u >= HEADS:
                    vec.wait_ge(u_ready, u - HEADS + 1)
                nc.vector.reciprocal(rinv[:, h:h + 1], rsum[:, h:h + 1]).then_inc(rinv_ready, 1)

            def u_sum(v, h):
                if not isinstance(v, int) or v >= 1:
                    vec.wait_ge(u_transposed, v)
                vec.wait_ge(half_ready, v + 1)
                nc.vector.scalar_tensor_tensor(U[:, :], ACC[h % 2][:, 0:F], rinv[:, h:h + 1], UH[:, :],
                                               ALU.mult, ALU.add).then_inc(u_ready, 1)

            def ut_low(v, h):
                vec.wait_ge(ut_hi_ready, v + 1)
                nc.vector.tensor_tensor(UT[:, 1, :], PU[h % 2], UT[:, 0, :], ALU.subtract).then_inc(ut_lo_ready, 1)

            def mask(ib):
                vec.wait_ge(mask_in, 16 * (ib + 1))
                nc.vector.tensor_scalar(AT[:, :, bass.ds(ib * P, P)], MT[:, :, :], 1.0, None,
                                        ALU.mult).then_inc(mask_ready, 1)

            def x1_sum(b):
                vec.wait_ge(xres_in, 16 * (b + 1))
                vec.wait_ge(w_multiplied, 4 * b + 4)
                if not isinstance(b, int) or b >= 1:
                    vec.wait_ge(x1_stored, 16 * b)
                nc.vector.tensor_tensor(X1[:, :], PO[:, 0:F], XR[:, :], ALU.add).then_inc(x1_ready, 1)

            def x1_stats(b):
                vec.wait_ge(x1_ready, b + 1)
                nc.vector.bn_stats(stat[:, :], X1[:, :]).then_inc(stat_ready, 1)
                vec.wait_ge(stat_ready, b + 1)
                if not isinstance(b, int):
                    vec.sem_inc(passed_vec, 1)
                nc.vector.bn_aggr(mv[:, :], stat[:, :]).then_inc(mv_ready, 1)

            def norm1(b):
                vec.wait_ge(rstd_ready, b + 1)
                if not isinstance(b, int) or b >= 1:
                    vec.wait_ge(h1_transposed, b)
                nc.vector.tensor_scalar(HN1[:, :], X1[:, :], mv[:, 0:1], rstd[:, 0:1], ALU.subtract, ALU.mult)\
                    .then_inc(norm1_ready, 1)

            def hidden(b):
                if isinstance(b, int) and b == NB - 1:
                    vec.wait_ge(hid_lo_ready, 4)
                elif not isinstance(b, int) or b >= 1:
                    vec.wait_ge(hid_stored, 16 * b)
                vec.wait_ge(hid_summed, b + 1)
                nc.vector.tensor_tensor(HID[:, :], PG, B1[:, :], ALU.add).then_inc(hid_ready, 1)

            def slot(ib, h):
                u = 4 * ib + h
                if has(u - 2):
                    ut_low(u - 2, (h - 2) % 4)
                if has(u - 1):
                    u_sum(u - 1, (h - 1) % 4)
                if h == 2 and (not isinstance(ib, int) or ib >= 2):
                    hidden(ib - 2)
                if h == 2 and (not isinstance(ib, int) or ib >= 1):
                    x1_stats(ib - 1)
                if h == 3 and (not isinstance(ib, int) or ib >= 1):
                    norm1(ib - 1)
                early = isinstance(u, int) and u < 2
                if not early and has(u + 4):
                    logits(u + 4, h)
                if has(u + 2):
                    low(u + 2, 2 * ib + (h + 2) // 2, (h + 2) % 4)
                if has(u + 3):
                    row_inverse(u + 3, (h + 3) % 4)
                if early:
                    logits(u + 4, h)
                if h == (1 if isinstance(ib, int) and ib == 0 else 0) and not final(ib):
                    mask_rows(ib + 1)
                if h == 1 and (not isinstance(ib, int) or ib >= 1):
                    x1_sum(ib - 1)
                if h == 3 and not final(ib):
                    mask(ib + 1)
                if final(ib) and h == 1:
                    degree(0)
                if final(ib) and h == 2:
                    for n in range(2):
                        hidden_low(n + 1, *PARTS[n], HIN[:, PARTS[n][0]:PARTS[n][1], :])
                if final(ib) and h == 3:
                    degree(1)
                    degree(2)

            def degree(ib):
                nc.vector.tensor_reduce(deg[:, bass.ds(ib, 1)], AT[:, bass.ds(ib, 1), :], mybir.AxisListType.XY,
                                        ALU.add).then_inc(deg_ready, 1)
                vec.wait_ge(deg_ready, ib + 1)
                if not isinstance(ib, int):
                    vec.sem_inc(passed_vec, 1)
                nc.vector.reciprocal(rdeg[:, bass.ds(ib, 1)], deg[:, bass.ds(ib, 1)]).then_inc(rdeg_ready, 1)

            def hidden_low(n, lo, hi, rows):
                vec.wait_ge(hid_hi_ready, n)
                nc.vector.tensor_tensor(HS[:, lo:hi, F:2 * F], rows, HS[:, lo:hi, 0:F],
                                        ALU.subtract).then_inc(hid_lo_ready, 1)

            vec.wait_ge(w_lo_ready, 1)
            adj_dst(0)
            logits(0, 0)
            adj_dst(1)
            row_inverse(0, 0)
            logits(1, 1)
            low(0, 0, 0)
            logits(2, 2)
            row_inverse(1, 1)
            low(1, 0, 1)
            logits(3, 3)
            row_inverse(2, 2)
            mask(0)

            def body(ib):
                for h in range(HEADS):
                    slot(ib, h)
            block_loop(vec, body)
            ut_low(UNITS - 2, 2)
            u_sum(UNITS - 1, 3)
            hidden(NB - 2)
            hidden_low(3, *PARTS[2], HIN[:, EARLY:BACK, :])
            ut_low(UNITS - 1, 3)
            hidden_low(4, NB - 2, NB - 1, HID[:, :].rearrange("p (b f) -> p b f", b=1))
            x1_sum(NB - 1)
            x1_stats(NB - 1)
            norm1(NB - 1)
            hidden(NB - 1)
            hidden_low(5, NB - 1, NB, HID[:, :].rearrange("p (b f) -> p b f", b=1))

            def finish(ib, j):
                if not isinstance(ib, int) or ib >= 2:
                    vec.wait_ge(out_stored[j % 2], 8 * (ib - j % 2))
                vec.wait_ge(rdeg_ready, ib + 1)
                vec.wait_ge(half_x1_ready, ib + 1)
                if not isinstance(ib, int):
                    vec.sem_inc(passed_vec, 1)
                nc.vector.scalar_tensor_tensor(OUT[:, j % 2, :], AC[j][:, 0:F], rdeg[:, bass.ds(ib, 1)], OX[:, j, :],
                                               ALU.mult, ALU.add).then_inc(out_ready, 1)

            for j in range(BUFS):
                finish(j, j)
                degree(j + 3)
            with vec.Fori(1, NB // BUFS - 1) as quad:
                for j in range(BUFS):
                    finish(BUFS * quad + j, j)
                    degree(BUFS * quad + j + 3)
            for j in range(BUFS):
                finish(NB - BUFS + j, j)
                if j == 0:
                    degree(NB - 1)



_INS = ["x", "adj", "L0_gnn_W", "L0_gnn_a", "L1_gnn_W", "L1_gnn_b"]


def kernel(**inputs):
    import numpy as np
    import concourse.bacc as bacc
    from concourse.bass_utils import run_bass_kernel_spmd

    nc = bacc.Bacc("TRN2", target_bir_lowering=False, num_devices=1)
    arrays, args = {}, []
    for name in _INS:
        a = np.ascontiguousarray(inputs[name])
        arrays["in_" + name] = a
        args.append(nc.dram_tensor("in_" + name, a.shape, mybir.dt.from_np(a.dtype), kind="ExternalInput").ap())
    out = nc.dram_tensor("out_0", (N, F), mybir.dt.float32, kind="ExternalOutput").ap()
    gnn_kernel(nc, *args, out)
    return run_bass_kernel_spmd(nc, [arrays], core_ids=[0]).results[0]["out_0"]
```
